# Optimizing a Trainium2 kernel written in Bass

```python
import numpy as np
import jax
import jax.numpy as jnp

def _softmax(x, axis=-1):
    return jax.nn.softmax(x, axis=axis)

def _gelu(x):
    return jax.nn.gelu(x, approximate=True)

def _silu(x):
    return jax.nn.silu(x)

def _sigmoid(x):
    return jax.nn.sigmoid(x)

def _layernorm(x, axis=-1, eps=1e-05):
    m = jnp.mean(x, axis=axis, keepdims=True)
    v = jnp.var(x, axis=axis, keepdims=True)
    return (x - m) / jnp.sqrt(v + eps)

def _scatter_add(tgt, idx, src, axis=0):
    return tgt.at[idx].add(src)

def _segment_sum(src, seg, n):
    return jax.ops.segment_sum(src, seg, n)
kernel_name = 'mk_pixart_resid_d1_seqx_r4_3f8715'

def setup_inputs(seed: int=0):
    np.random.seed(seed)
    _w = jnp.asarray

    def _rec_inputs():
        import jax
        import jax.numpy as jnp
        _rk = jax.random.key(seed)
        x = -0.0002928 + 1 * jax.random.normal(jax.random.fold_in(_rk, 1), (16, 128, 256), jnp.float32)
        _lenS = 128 - jax.random.randint(jax.random.fold_in(_rk, 7), (16,), 0, max(1, 128 // 4) + 1, jnp.int32)
        _lenS2 = 128 - jax.random.randint(jax.random.fold_in(_rk, 8), (16,), 0, max(1, 128 // 4) + 1, jnp.int32)
        _ctx_1024P = jax.random.normal(jax.random.fold_in(_rk, 11), (16, 16, 256), jnp.float32)
        _ctx_1024c = jax.random.dirichlet(jax.random.fold_in(_rk, 511), 0.3 * jnp.ones((16,), jnp.float32), (16, 128))
        _ctx_1024t = jnp.einsum('bsk,bkd->bsd', _ctx_1024c, _ctx_1024P)
        _ctx_1024t = _ctx_1024t * jax.lax.rsqrt(jnp.mean(jnp.square(_ctx_1024t)) + 1e-12) * 0.953939
        ctx_1024 = -1.39393e-06 + 0.999914 * (_ctx_1024t + 0.3 * jax.random.normal(jax.random.fold_in(_rk, 611), (16, 128, 256), jnp.float32))
        condB_tau = jax.random.uniform(jax.random.fold_in(_rk, 12), (16,), jnp.float32, 0.0, 1.23395)
        fside_BxS2_0 = -0.00205293 + 0.99739 * jax.random.normal(jax.random.fold_in(_rk, 13), (16, 128), jnp.float32)
        return (x, ctx_1024, condB_tau, fside_BxS2_0)
    x, ctx_1024, condB_tau, fside_BxS2_0 = _rec_inputs()

    def _L0_xcond_setup():
        import jax, jax.numpy as jnp
        import numpy as np
        B, S, D, H = (2, 512, 256, 16)
        DK = D // H

        def _split_heads(x):
            b, s, _ = x.shape
            return x.reshape(b, s, H, DK).transpose(0, 2, 1, 3)
        key = jax.random.key(seed)
        ks = jax.random.split(key, 14)
        inp = {'query': jax.random.normal(ks[0], (B, S, D), jnp.float32), 'key': jax.random.normal(ks[1], (B, S, D), jnp.float32), 'value': jax.random.normal(ks[2], (B, S, D), jnp.float32), 'tau': jax.random.uniform(ks[3], (B, 1), jnp.float32, 0.5, 1.5), 'delta': jax.random.normal(ks[4], (B, S), jnp.float32)}
        sc = 1.0 / np.sqrt(D)
        for i, name in enumerate(['q', 'k', 'v', 'o']):
            inp[f'W{name}'] = jax.random.normal(ks[5 + 2 * i], (D, D), jnp.float32) * sc
            inp[f'b{name}'] = jax.random.normal(ks[6 + 2 * i], (D,), jnp.float32) * 0.01
        return inp
    _L0_xcond_all = _L0_xcond_setup()
    _L0_xcond_in = {k: v for k, v in _L0_xcond_all.items() if k in ('Wq', 'bq', 'Wk', 'bk', 'Wv', 'bv', 'Wo', 'bo')}
    del _L0_xcond_all

    def _L0_ffn_setup():
        import jax, jax.numpy as jnp
        import numpy as np
        E = 8
        K = 2
        D = 256
        P = 1024
        key = jax.random.key(seed)
        ks = jax.random.split(key, 8)
        s = lambda fan_in: 1.0 / np.sqrt(fan_in)
        x = jax.random.normal(ks[0], (2, 512, D), dtype=jnp.float32)
        W1 = jax.random.normal(ks[1], (E, D, P), dtype=jnp.float32) * s(D)
        b1 = jax.random.normal(ks[2], (E, P), dtype=jnp.float32) * 0.01
        W2 = jax.random.normal(ks[3], (E, P, D), dtype=jnp.float32) * s(P)
        b2 = jax.random.normal(ks[4], (E, D), dtype=jnp.float32) * 0.01
        Wr = jax.random.normal(ks[5], (D, E), dtype=jnp.float32) * s(D)
        br = jax.random.normal(ks[6], (E,), dtype=jnp.float32) * 0.01
        return {'x': x, 'W1': W1, 'b1': b1, 'W2': W2, 'b2': b2, 'Wr': Wr, 'br': br}
    _L0_ffn_all = _L0_ffn_setup()
    _L0_ffn_in = {k: v for k, v in _L0_ffn_all.items() if k in ('W1', 'b1', 'W2', 'b2', 'Wr', 'br')}
    del _L0_ffn_all
    return {'x': x, 'ctx_1024': ctx_1024, 'condB_tau': condB_tau, 'fside_BxS2_0': fside_BxS2_0, 'L0_xcond_Wq': _L0_xcond_in['Wq'], 'L0_xcond_bq': _L0_xcond_in['bq'], 'L0_xcond_Wk': _L0_xcond_in['Wk'], 'L0_xcond_bk': _L0_xcond_in['bk'], 'L0_xcond_Wv': _L0_xcond_in['Wv'], 'L0_xcond_bv': _L0_xcond_in['bv'], 'L0_xcond_Wo': _L0_xcond_in['Wo'], 'L0_xcond_bo': _L0_xcond_in['bo'], 'L0_ffn_W1': _L0_ffn_in['W1'], 'L0_ffn_b1': _L0_ffn_in['b1'], 'L0_ffn_W2': _L0_ffn_in['W2'], 'L0_ffn_b2': _L0_ffn_in['b2'], 'L0_ffn_Wr': _L0_ffn_in['Wr'], 'L0_ffn_br': _L0_ffn_in['br']}

def reference(x, ctx_1024, condB_tau, fside_BxS2_0, L0_xcond_Wq, L0_xcond_bq, L0_xcond_Wk, L0_xcond_bk, L0_xcond_Wv, L0_xcond_bv, L0_xcond_Wo, L0_xcond_bo, L0_ffn_W1, L0_ffn_b1, L0_ffn_W2, L0_ffn_b2, L0_ffn_Wr, L0_ffn_br):
    import jax
    import jax.numpy as jnp

    def _L0_xcond_ref(query, key, value, tau, delta, Wq, bq, Wk, bk, Wv, bv, Wo, bo):
        import jax, jax.numpy as jnp
        import numpy as np
        B, S, D, H = (2, 512, 256, 16)
        DK = D // H

        def _split_heads(x):
            b, s, _ = x.shape
            return x.reshape(b, s, H, DK).transpose(0, 2, 1, 3)
        q = _split_heads(query @ Wq.T + bq)
        k = _split_heads(key @ Wk.T + bk)
        v = _split_heads(value @ Wv.T + bv)
        scores = jnp.einsum('bhqd,bhkd->bhqk', q, k)
        scores = scores * tau[:, :, None, None] + delta[:, None, None, :]
        scores = scores / jnp.sqrt(jnp.asarray(DK, scores.dtype))
        p_attn = jax.nn.softmax(scores, axis=-1)
        x = jnp.einsum('bhqk,bhkd->bhqd', p_attn, v)
        x = x.transpose(0, 2, 1, 3).reshape(query.shape[0], -1, H * DK)
        return x @ Wo.T + bo

    def _L0_ffn_ref(x, W1, b1, W2, b2, Wr, br):
        import jax, jax.numpy as jnp
        import numpy as np
        E = 8
        K = 2
        D = 256
        P = 1024
        B, S, _ = x.shape
        xf = x.reshape(B * S, D)
        scores = xf @ Wr + br
        _, top_idx = jax.lax.top_k(scores, K)
        mask = jax.nn.one_hot(top_idx, E, dtype=scores.dtype).sum(-2) > 0
        router_weights = jax.nn.softmax(jnp.where(mask, scores, -jnp.inf), axis=-1)
        h = jax.nn.gelu(jnp.einsum('td,edp->etp', xf, W1) + b1[:, None, :])
        y = jnp.einsum('etp,epd->etd', h, W2) + b2[:, None, :]
        out = jnp.einsum('te,etd->td', router_weights, y)
        return out.reshape(B, S, D)
    x = x + _L0_xcond_ref(_layernorm(x, axis=-1), ctx_1024, ctx_1024, condB_tau[:, None], fside_BxS2_0, L0_xcond_Wq, L0_xcond_bq, L0_xcond_Wk, L0_xcond_bk, L0_xcond_Wv, L0_xcond_bv, L0_xcond_Wo, L0_xcond_bo)
    x = x + _L0_ffn_ref(_layernorm(x, axis=-1), L0_ffn_W1, L0_ffn_b1, L0_ffn_W2, L0_ffn_b2, L0_ffn_Wr, L0_ffn_br)
    return x

_drawn_inputs = setup_inputs


def setup_inputs(seed=0):
    import zlib

    import numpy as np

    out = dict(_drawn_inputs(seed))
    spreads = {}
    factors = {'L0_xcond_bq': 7.725, 'L0_xcond_bk': 8.0, 'L0_ffn_b1': 8.0, 'L0_ffn_b2': 8.0}
    for name, (base, spread) in spreads.items():
        noise = np.random.default_rng([zlib.crc32(name.encode()), seed]).standard_normal(out[name].shape)
        drawn = base * np.exp(spread * noise) if base else spread * noise
        out[name] = jnp.asarray(drawn.astype(out[name].dtype))
    for name, factor in factors.items():
        out[name] = (out[name] * factor).astype(out[name].dtype)
    return out
```

```python
import concourse.bass as bass
from concourse import mybir
from contextlib import ExitStack

P = 128
B, S, D = 16, 128, 256
KT = D // P
H, DK = 16, 16
E, F = 8, 1024
FC = F // P
T = B * S
G = B // 2
NT = (2 * T - E) // P + E
EPS = 1e-5

fp32 = mybir.dt.float32
fp16 = mybir.dt.float16
i32 = mybir.dt.int32
ALU = mybir.AluOpType
ACT = mybir.ActivationFunctionType
AX = mybir.AxisListType


def known(t):
    return isinstance(t, int)


def moe_block_kernel(nc, x, ctx_in, tau, side, Wq, bq, Wk, bk, Wv, bv, Wo, bo,
                     W1, b1, W2, b2, Wr, br, out):
    stack = ExitStack()
    with stack:
        def sb(name, shape, dt=fp32):
            return stack.enter_context(nc.sbuf_tensor(name, shape, dt))

        def sem(name):
            return stack.enter_context(nc.semaphore(name))

        qk_dram = nc.dram_tensor("qk_dram", (2, 4, D, 2 * S), fp16, kind="Internal").ap()
        delta_dram = nc.dram_tensor("delta_dram", (2, B, S), fp16, kind="Internal").ap()
        b2_dram = nc.dram_tensor("b2_dram", (2, E, D), fp16, kind="Internal").ap()
        xn2_dram = nc.dram_tensor("xn2_dram", (T + P, D), fp32, kind="Internal").ap()

        w1h = sb("w1h", [P, E * KT * F], fp16)
        w1l = sb("w1l", [P, E * KT * F], fp16)
        w2h = sb("w2h", [P, E * FC * D], fp16)
        w2l = sb("w2l", [P, E * FC * D], fp16)
        stage = sb("stage", [P, 2, 1024])
        wah = sb("wah", [P, 4, KT, D], fp16)
        wal = sb("wal", [P, 4, KT, D], fp16)
        wr = sb("wr", [P, KT, E])
        brb = sb("brb", [P, E])
        bvb = sb("bvb", [P, D])
        bob = sb("bob", [P, D])
        bcols = sb("bcols", [P, E * FC + 4])
        tau4 = sb("tau4", [P, B])
        tbq = sb("tbq", [P, KT, B])
        ident = sb("ident", [P, P])
        identh = sb("identh", [P, P], fp16)
        onesh = sb("onesh", [P, P], fp16)
        trih = sb("trih", [P, P], fp16)
        sel = sb("sel", [2 * H, H], fp16)
        nhalf = sb("nhalf", [P, 2])
        rev = sb("rev", [P, E])
        steps128 = sb("steps128", [P, B])
        notfirst = sb("notfirst", [P, E * B])
        tokval = sb("tokval", [P, 2, B], fp16)
        slot_no = sb("slot_no", [P, P], fp16)
        tile_no = sb("tile_no", [P, NT], fp16)
        part_no = sb("part_no", [P, 1])
        xin = sb("xin", [P, 2, D])
        cin = sb("cin", [P, 2, D])
        xn = sb("xn", [P, 2, D])
        xb = sb("xb", [P, 2, 2, D])
        st1 = sb("st1", [P, 2, 6])
        mv1 = sb("mv1", [P, 2, 2])
        rs1 = sb("rs1", [P, 3, 2])
        xT = sb("xT", [P, 4, KT, 2 * S], fp16)
        qk32 = sb("qk32", [P, KT, 2 * S])
        qkc = sb("qkc", [P, 4, KT, 2 * S], fp16)
        QS = sb("QS", [P, 2, H // 2, 2 * S], fp16)
        KS = sb("KS", [P, 2, H // 2, 2 * S], fp16)
        V = sb("V", [P, 2, 2, H, DK + 1])
        PT = sb("PT", [P, H, S])
        mx = sb("mx", [P, H])
        mm = sb("mm", [P, 2 * H], fp16)
        mT = sb("mT", [2 * H, S], fp16)
        rec = sb("rec", [P, H])
        on = sb("on", [P, H, DK])
        oT = sb("oT", [P, 2, KT, S], fp16)
        x1 = sb("x1", [P, 2, D])
        xn2 = sb("xn2", [P, 2, D])
        st2 = sb("st2", [P, 6])
        mv2 = sb("mv2", [P, 2])
        rs2 = sb("rs2", [P, 2])
        xn2T = sb("xn2T", [P, KT, S])
        sc = sb("sc", [P, E, B])
        rc = sb("rc", [P, 3, E])
        mask = sb("mask", [P, E * B], fp16)
        pos = sb("pos", [P, 2, B])
        posi = sb("posi", [P, 3, 2 * B], i32)
        posf = sb("posf", [P, 2, 2 * B], fp16)
        vals = sb("vals", [P, 3, 2 * B], fp16)
        slot_rows = sb("slot_rows", [P, NT], i32)
        slot_w = sb("slot_w", [P, NT])
        slot_t = sb("slot_t", [P, 2, NT])
        tile_f = sb("tile_f", [1, 2, NT])
        tile_exp = sb("tile_exp", [1, NT], i32)
        idxg = sb("idxg", [P, 2], i32)
        idxs = sb("idxs", [P, 1], i32)

        flatPT = PT[:, :, :].rearrange("p a b -> p (a b)")
        bias_rows = flatPT[:, 0:P]
        b2rows = flatPT[0:E, 128:384]
        delta = flatPT[0:B, 384:512]
        b2parts = flatPT[0:E, 512:768].bitcast(fp16).rearrange("p (r d) -> p r d", r=2)
        dparts = flatPT[0:B, 768:896].bitcast(fp16).rearrange("p (r s) -> p r s", r=2)
        flatxb = xb[:, :, :, :].rearrange("p a b d -> p (a b d)")
        hot = flatxb[:, 0:256].rearrange("p (c e b) -> p c e b", c=2, e=E)
        ra = flatxb[:, 256:640].rearrange("p (c e b) -> p c e b", c=3, e=E)
        rb = flatxb[:, 640:768].rearrange("p (c b) -> p c b", b=B)
        tile_e = xn[0:1, :, :].rearrange("p a d -> p (a d)")[:, 0:NT * E].rearrange("p (j e) -> p j e", e=E)
        hot_tile = KS[:, :, :, :].rearrange("p a b c -> p (a b c)")[:, 0:2 * B * NT]\
            .rearrange("p (i j) -> p i j", j=NT)
        b2r = V[0:2, :, :, :, :].rearrange("p a b h d -> p (a b h d)")[:, 0:E * D // 2].bitcast(fp16)
        hot_slot = flatPT.bitcast(fp16)\
            .rearrange("p (i r) -> p i r", r=P)
        hot_val = QS[:, :, :, :].rearrange("p a b c -> p (a b c)")[:, 0:2 * B * 3 * NT]\
            .rearrange("p (i v j) -> p i v j", v=3, j=NT)
        xs = xin
        hid = [PT[:, r * FC:(r + 1) * FC, :] for r in range(2)]
        hh, hl = [[q[:, r, 0:4, :].rearrange("p a n -> p (a n)") for r in range(2)] for q in (QS, KS)]
        yw = x1

        banks = [stack.enter_context(nc.psum_tensor(f"bank{i}", [P, 512], fp32)) for i in range(8)]
        psS, psST, pA, pB = banks[0:2], banks[2:4], banks[4], banks[5]
        pT6 = banks[6][:, 0:256].rearrange("p (k n) -> p k n", k=KT)
        pY6 = banks[6][:, 256:512]
        pO = banks[7][:, 0:H * (DK + 1)].rearrange("p (h d) -> p h d", d=DK + 1)
        pM = banks[7][:, 288:352].bitcast(fp16)
        pR = pY6[:, 0:E]

        names = """zeroed const_ready ones_ready bcols_loaded wa_loaded small_in
            wT_ps wT_hi wT_lo bc_ps bc_ready delta_split delta_stored b2_split b2_stored b2_moved
            zeros_stored w_lo
            ln1_stats rstd1 xb_ready xn_ready xT_ps cT_ps xh_ready ch_ready xl_ready cl_ready q_ps k_ps
            q32_ready k32_ready qh_ready kh_ready ql_ready kl_ready v_ps v_ready qk_stored
            s_ps m_red mm_ready mT_ps mT_ready st_ps exp_done po_ps on_ready oT_ps oh_ready ol_ready
            y_ps x1_ready ln2_stats rstd2 xn2_ready x2T_ps x2T_ready r_ps sc_ready
            c_setup c_pool c_ln1 c_rs1 c_mm c_on c_ln2 c_rs2 c_wsplit c_route
            mask_ready gap_ready e_ready rank_ps hot_ready slot_ps routed
            idxg_ready idxs_ready gT_ps gh_ready gl_ready h_ps gelu_done hh_done hl_done yy_ps yy_ready
            added""".split()
        s = {n: sem(n) for n in names}
        x_loaded, c_loaded = sem("x_loaded"), sem("c_loaded")
        stack_ready = [sem(f"stack_ready{i}") for i in range(2)]
        x1_stored = [sem(f"x1_stored{i}") for i in range(2)]
        xn2_stored = [sem(f"xn2_stored{i}") for i in range(2)]
        w_loaded = [sem(f"w_loaded{i}") for i in range(2)]
        rows_in = [sem(f"rows_in{i}") for i in range(2)]
        block = stack.enter_context(nc.Block())

        def wait(eng, name, n):
            if not known(n) or n > 0:
                eng.wait_ge(s[name] if isinstance(name, str) else name, n)

        def own_wait(eng, name, n):
            if known(n):
                eng.wait_ge(s[name], n)
            else:
                n = eng.to_reg(n)
                eng.wait_ge(s["const_ready"], 1)
                eng.wait_ge(s[name], n)

        def chain(eng, name, base=0):
            k = [0]

            def link(ins):
                k[0] += 1
                ins.then_inc(s[name], 1)
                eng.wait_ge(s[name], base + k[0])
            return link

        def attention_steps(eng, step):
            step(0, 0)
            step(1, 1)
            with eng.Fori(1, 3) as i:
                step(i * 2, 0)
                step(i * 2 + 1, 1)
            for t in (6, 7, 8):
                step(t, t % 2)

        def expert_steps(eng, step):
            for t in range(4):
                step(t, t % 2)
            with eng.Fori(2, (NT - 3) // 2) as i:
                step(i * 2, 0)
                step(i * 2 + 1, 1)
            for t in range(NT - 3, NT + 2):
                step(t, t % 2)

        def has(t, lo, hi):
            return not known(t) or lo <= t < hi

        ROWS = 3 * DK + 2

        def unit_heads(u):
            return slice(8 * (u // 2) + u % 2, 8 * (u // 2) + 8, 2)

        @block.sync
        def _(sp):
            def load_x(g):
                wait(sp, "xb_ready", g)
                sp.dma_start(xin[:, :, :], x[bass.ds(g * 2, 2), :, :].rearrange("b s d -> s b d"))\
                  .then_inc(x_loaded, 16)

            def load_ctx(g):
                own_wait(sp, "cT_ps", g)
                sp.dma_start(cin[:, :, :], ctx_in[bass.ds(g * 2, 2), :, :].rearrange("b s d -> s b d"))\
                  .then_inc(c_loaded, 16)

            def load_w(e, n):
                wait(sp, "w_lo", 4 * e + n - 1)
                if n < 2:
                    src = W1[bass.ds(e, 1), n * P:(n + 1) * P, :].rearrange("e p n -> p (e n)")
                    dst = stage[:, n % 2, :]
                else:
                    src = W2[bass.ds(e, 1), (n - 2) * 512:(n - 1) * 512, :]\
                        .rearrange("e (c p) d -> p (e c) d", p=P)
                    dst = stage[:, n % 2, :].rearrange("p (c d) -> p c d", d=D)
                sp.dma_start(dst, src).then_inc(w_loaded[n % 2], 16)

            def rows(v):
                return v.rearrange("(a n) -> a n", a=1)

            load_x(0)
            load_ctx(0)
            for n, w in enumerate((Wq, Wk, Wv, Wo)):
                sp.dma_start(stage[:, n // 2, (n % 2) * 512:(n % 2 + 1) * 512].rearrange("p (a i) -> p a i", i=D),
                             w.rearrange("(a p) i -> p a i", p=P)).then_inc(s["wa_loaded"], 16)
            sp.dma_start(bias_rows[0:64, :], b1.rearrange("e (c p) -> (e c) p", p=P)).then_inc(s["bcols_loaded"], 16)
            sp.dma_start(bias_rows[64:66, :], bq.rearrange("(c p) -> c p", p=P)).then_inc(s["bcols_loaded"], 16)
            sp.dma_start(bias_rows[66:68, :], bk.rearrange("(c p) -> c p", p=P)).then_inc(s["bcols_loaded"], 16)
            sp.dma_start(delta, side).then_inc(s["small_in"], 16)
            sp.dma_start(b2rows, b2).then_inc(s["small_in"], 16)
            sp.dma_start(wr[:, :, :], Wr.rearrange("(k p) e -> p k e", p=P)).then_inc(s["small_in"], 16)
            for dst, src, n in ((tau4, tau, B), (brb, br, E), (bvb, bv, D), (bob, bo, D)):
                sp.dma_start(dst[:, :], rows(src).to_broadcast([P, n])).then_inc(s["small_in"], 16)
            sp.wait_ge(s["delta_split"], 1)
            for r in range(2):
                sp.dma_start(delta_dram[r], dparts[:, r, :]).then_inc(s["delta_stored"], 16)
            sp.wait_ge(s["b2_split"], 1)
            for r in range(2):
                sp.dma_start(b2_dram[r], b2parts[:, r, :]).then_inc(s["b2_stored"], 16)
            sp.wait_ge(s["zeroed"], 1)
            sp.dma_start(xn2_dram[T:T + P, :], xn2[:, 0, :]).then_inc(s["zeros_stored"], 16)
            sp.dma_start(out[T:T + P, :], xn2[:, 0, :]).then_inc(s["zeros_stored"], 16)
            sp.wait_ge(s["b2_stored"], 32)
            sp.wait_ge(s["delta_stored"], 32)
            sp.wait_ge(s["wT_ps"], 4)
            load_w(0, 0)
            load_w(0, 1)

            def put_rows(b, bb):
                sp.wait_ge(s["x1_ready"], b + 1)
                sp.dma_start(out[bass.ds(b * S, S), :], x1[:, bb, :]).then_inc(x1_stored[bb], 16)
                sp.wait_ge(s["xn2_ready"], b + 1)
                sp.dma_start(xn2_dram[bass.ds(b * S, S), :], xn2[:, bb, :]).then_inc(xn2_stored[bb], 16)

            def step(t, p):
                if has(t, 2, G + 1):
                    put_rows(2 * t - 3, 1)
                if has(t, 0, G - 1):
                    load_ctx(t + 1)
                    load_x(t + 1)
                if has(t, 0, G):
                    sp.wait_ge(s["ql_ready"], t + 1)
                    sp.wait_ge(s["kl_ready"], t + 1)
                    for n in range(4):
                        sp.dma_start(qk_dram[p, n].rearrange("(c p) n -> p c n", p=P), qkc[:, n, :, :])\
                          .then_inc(s["qk_stored"], 16)
                    own_wait(sp, "qk_stored", 64 * (t + 1))
                    wait(sp, "st_ps", 8 * (t - 1))
                    sp.wait_ge(s["ones_ready"], 1)
                    for n, dst in enumerate((QS, KS)):
                        for par in range(2):
                            for k, part in enumerate(((0, 0, 1), (2, 3, 2))[n]):
                                src = qk_dram[p, part].rearrange("(j a i) n -> a i j n", a=2, i=DK)[par]
                                r = 64 * par + DK * k
                                sp.dma_start(dst[r:r + DK, p, :, :], src).then_inc(stack_ready[p], 16)
                    for par in range(2):
                        r = 64 * par + 3 * DK
                        src = delta_dram[:, bass.ds(t * 2, 2), :].rearrange("r b n -> r (b n)")
                        sp.dma_start(KS[r:r + 2, p, :, :],
                                     src.unsqueeze(1).to_broadcast([2, H // 2, 2 * S]))\
                          .then_inc(stack_ready[p], 16)
                if has(t, 0, E):
                    load_w(t, 2)
                    load_w(t, 3)
                if has(t, 1, G + 1):
                    put_rows(2 * t - 2, 0)
                if has(t, 0, E - 1):
                    load_w(t + 1, 0)
                    load_w(t + 1, 1)

            attention_steps(sp, step)
            put_rows(B - 1, 1)
            sp.wait_ge(s["po_ps"], B)
            sp.dma_start(b2r, b2_dram.rearrange("r e d -> r (e d)")).then_inc(s["b2_moved"], 16)

        @block.gpsimd
        def _(pool):
            link = chain(pool, "c_pool")
            for m in (ident, identh, trih):
                pool.memset(m[:, :], 0.0)
            pool.memset(sel[:, :], 0.0)
            pool.memset(onesh[:, :], 1.0)
            pool.memset(nhalf[:, :], -0.5)
            link(pool.memset(notfirst[:, :], 1.0))
            for m in (ident, identh):
                link(pool.affine_select(out=m[:, :], in_=m[:, :], compare_op=ALU.not_equal, fill=1.0,
                                        base=0, pattern=[[-1, P]], channel_multiplier=1))
            link(pool.affine_select(out=trih[:, :], in_=trih[:, :], compare_op=ALU.is_ge, fill=1.0,
                                    base=0, pattern=[[-1, P]], channel_multiplier=1))
            for base in (0, -H):
                link(pool.affine_select(out=sel[:, :], in_=sel[:, :], compare_op=ALU.not_equal,
                                        fill=1.0, base=base, pattern=[[-1, H]],
                                        channel_multiplier=1))
            link(pool.affine_select(out=notfirst[:, :], in_=notfirst[:, :], compare_op=ALU.not_equal,
                                    fill=0.0, base=0, pattern=[[0, E], [1, B]], channel_multiplier=0))

            def iota(dst, pattern, base, mult):
                return pool.iota(dst, pattern, base=base, channel_multiplier=mult,
                                 allow_small_or_imprecise_dtypes=True)

            iota(rev[:, :], [[-1, E]], E, 0)
            iota(steps128[:, :], [[P, B]], 0, 0)
            iota(tokval[:, :, :], [[0, 2], [S, B]], -T, 1)
            iota(slot_no[:, :], [[1, P]], 0, 0)
            iota(tile_no[:, :], [[1, NT]], 0, 0)
            iota(part_no[:, :], [[0, 1]], 0, 1).then_inc(s["const_ready"], 1)

            def split_piece(e, n):
                h, l = ((w1h, w1l), (w2h, w2l))[n // 2]
                at = bass.ds(e * (KT * F) + (n % 2) * 1024, 1024)
                pool.wait_ge(w_loaded[n % 2], 32 * e + 16 * (n // 2 + 1))
                pool.tensor_copy(h[:, at], stage[:, n % 2, :]).then_inc(s["c_wsplit"], 1)
                pool.wait_ge(s["c_wsplit"], 4 * e + n + 1)
                pool.tensor_tensor(l[:, at], stage[:, n % 2, :], h[:, at], ALU.subtract).then_inc(s["w_lo"], 1)

            def rstd_1(g):
                link = chain(pool, "c_rs1", g)
                own_wait(pool, "ln1_stats", g + 1)
                link(pool.tensor_scalar(rs1[:, 0, :], mv1[:, :, 1], EPS, None, ALU.add))
                pool.tensor_tensor(rs1[:, 1, :], rs1[:, 0, :], nhalf[:, :], ALU.pow).then_inc(s["rstd1"], 1)

            def rstd_2(b):
                link = chain(pool, "c_rs2", b)
                own_wait(pool, "ln2_stats", b + 1)
                link(pool.tensor_scalar(rs2[:, 0:1], mv2[:, 1:2], EPS, None, ALU.add))
                pool.tensor_tensor(rs2[:, 1:2], rs2[:, 0:1], nhalf[:, 0:1], ALU.pow).then_inc(s["rstd2"], 1)

            rstd_1(0)

            def step(t, p):
                if has(t, 0, G):
                    split_piece(t, 0)
                if has(t, 2, G + 1):
                    rstd_2(2 * t - 3)
                if has(t, 0, G):
                    split_piece(t, 1)
                if has(t, 1, G + 1):
                    rstd_2(2 * t - 2)
                if has(t, 0, G - 1):
                    rstd_1(t + 1)
                if has(t, 0, G):
                    split_piece(t, 2)
                    split_piece(t, 3)

            attention_steps(pool, step)
            rstd_2(B - 1)

            pool.wait_ge(s["routed"], 1)
            pool.wait_ge(s["zeros_stored"], 32)
            for i in range(2):
                pool.wait_ge(x1_stored[i], 16 * G)
                pool.wait_ge(xn2_stored[i], 16 * G)

            def gather(j, p):
                wait(pool, "gT_ps", j - 1)
                pool.tensor_copy(idxg[:, p:p + 1], slot_rows[:, bass.ds(j, 1)]).then_inc(s["idxg_ready"], 1)
                own_wait(pool, "idxg_ready", j + 1)
                pool.indirect_dma_start(out=xs[:, p, :], out_offset=None, in_=xn2_dram,
                                        in_offset=bass.IndirectOffsetOnAxis(ap=idxg[:, p:p + 1], axis=0))\
                    .then_inc(rows_in[p], 16)

            def scatter(j, p):
                pool.wait_ge(s["yy_ready"], j + 1)
                wait(pool, "added", 16 * j)
                pool.tensor_copy(idxs[:, :], slot_rows[:, bass.ds(j, 1)]).then_inc(s["idxs_ready"], 1)
                own_wait(pool, "idxs_ready", j + 1)
                pool.indirect_dma_start(out=out, out_offset=bass.IndirectOffsetOnAxis(ap=idxs[:, :], axis=0),
                                        in_=yw[:, p, :], in_offset=None, compute_op=ALU.add)\
                    .then_inc(s["added"], 16)

            gather(0, 0)
            gather(1, 1)

            def step(t, p):
                if has(t, 0, NT - 2):
                    gather(t + 2, p)
                if has(t, 2, NT + 2):
                    scatter(t - 2, p)

            expert_steps(pool, step)
            pool.wait_ge(s["added"], 16 * NT)

        @block.scalar
        def _(act):
            def copy(dst, src):
                return act.activation(dst, src, ACT.Copy)

            for n in range(4):
                act.wait_ge(s["wT_ps"], n + 1)
                copy(wah[:, n, :, :], banks[n][:, :].rearrange("p (k n) -> p k n", k=KT)).then_inc(s["wT_hi"], 1)
            act.wait_ge(s["bc_ps"], 1)
            copy(bcols[:, :], pA[:, 0:E * FC + 4]).then_inc(s["bc_ready"], 1)

            def turned_hi(g):
                act.wait_ge(s["xT_ps"], g + 1)
                copy(xT[:, 0, :, :], pA[:, :].rearrange("p (k n) -> p k n", k=KT)).then_inc(s["xh_ready"], 1)
                act.wait_ge(s["cT_ps"], g + 1)
                copy(xT[:, 2, :, :], pB[:, :].rearrange("p (k n) -> p k n", k=KT)).then_inc(s["ch_ready"], 1)

            def qk_hi(g):
                wait(act, "qk_stored", 64 * g)
                for n, ready, done in ((0, "q32_ready", "qh_ready"), (2, "k32_ready", "kh_ready")):
                    act.wait_ge(s[ready], g + 1)
                    copy(qkc[:, n, :, :], qk32[:, :, :]).then_inc(s[done], 1)

            def exps(b):
                wait(act, "po_ps", b)
                for u in range(4):
                    act.wait_ge(s["st_ps"], 4 * b + u + 1)
                    act.activation(PT[:, unit_heads(u), :],
                                   psST[u % 2][:, :].rearrange("p (h n) -> p h n", h=4), ACT.Exp)\
                        .then_inc(s["exp_done"], 1)

            def oT_hi(b):
                act.wait_ge(s["oT_ps"], b + 1)
                copy(oT[:, 0, :, :], pT6).then_inc(s["oh_ready"], 1)

            def xn2_T(b):
                act.wait_ge(s["x2T_ps"], b + 1)
                copy(xn2T[:, :, :], pT6).then_inc(s["x2T_ready"], 1)

            def step(t, p):
                for bb in range(2):
                    b = 2 * t - 2 + bb
                    prev = has(t, 2 - bb, G + 1)
                    if prev:
                        oT_hi(b - 1)
                    if bb == 0 and has(t, 0, G):
                        turned_hi(t)
                    if has(t, 1, G + 1):
                        act.wait_ge(s["mT_ps"], b + 1)
                        copy(mT[:, :], pM[0:2 * H, :]).then_inc(s["mT_ready"], 1)
                        exps(b)
                    if prev:
                        xn2_T(b - 1)
                    if bb == 0 and has(t, 0, G):
                        qk_hi(t)

            attention_steps(act, step)
            oT_hi(B - 1)
            xn2_T(B - 1)

            act.wait_ge(s["gap_ready"], 1)
            act.activation(rb[:, 5, :], rb[:, 4, :], ACT.Exp).then_inc(s["e_ready"], 1)
            act.wait_ge(s["routed"], 1)

            def step(t, p):
                if has(t, 0, NT):
                    act.wait_ge(s["gT_ps"], t + 1)
                    copy(xT[:, 2 * p, :, 0:P], (pA, pB)[p][:, 0:KT * P].rearrange("p (k n) -> p k n", k=KT))\
                        .then_inc(s["gh_ready"], 1)
                if has(t, 1, NT + 1):
                    j, q = t - 1, 1 - p
                    wait(act, "hl_done", j - 1)
                    e = act.value_load(tile_exp[0:1, bass.ds(j, 1)], min_val=0, max_val=E - 1)
                    for c in range(FC):
                        if c % 4 == 0:
                            act.wait_ge(s["h_ps"], 2 * j + c // 4 + 1)
                        ins = act.activation(hid[q][:, c, :], banks[2 * q + c // 4][:, (c % 4) * P:(c % 4 + 1) * P],
                                             ACT.Gelu_apprx_tanh, bias=bcols[:, bass.ds(e * FC + c, 1)])
                    ins.then_inc(s["gelu_done"], 1)

            expert_steps(act, step)

        @block.vector
        def _(dve):
            V_ = V[:, :, :, :, :]
            link = chain(dve, "c_setup")
            dve.memset(xn2[:, 0, :], 0.0).then_inc(s["zeroed"], 1)
            dve.memset(V_[:, :, :, :, DK], 1.0)
            dve.memset(QS[:, :, :, :], 1.0).then_inc(s["ones_ready"], 1)
            dve.wait_ge(s["small_in"], 16 * 7)
            link(dve.tensor_scalar(tau4[:, :], tau4[:, :], DK ** -0.5, None, ALU.mult))
            link(dve.tensor_scalar(delta, delta, DK ** -0.5, None, ALU.mult))
            link(dve.tensor_copy(dparts[:, 0, :], delta))
            dve.tensor_tensor(dparts[:, 1, :], delta, dparts[:, 0, :], ALU.subtract)\
                .then_inc(s["delta_split"], 1)
            link(dve.tensor_copy(b2parts[:, 0, :], b2rows))
            dve.tensor_tensor(b2parts[:, 1, :], b2rows, b2parts[:, 0, :], ALU.subtract)\
                .then_inc(s["b2_split"], 1)
            dve.wait_ge(s["zeros_stored"], 32)

            def ln_1(g, p):
                dve.wait_ge(x_loaded, 16 * (g + 1))
                for i in range(2):
                    ins = dve.bn_stats(st1[:, i, :], xin[:, i, :])
                ins.then_inc(s["c_ln1"], 1)
                own_wait(dve, "c_ln1", 2 * g + 1)
                for i in range(2):
                    ins = dve.bn_aggr(mv1[:, i, :], st1[:, i, :])
                ins.then_inc(s["ln1_stats"], 1)
                dve.wait_ge(s["rstd1"], g + 1)
                dve.tensor_tensor(rs1[:, 2, :], rs1[:, 1, :], tau4[:, bass.ds(g * 2, 2)], ALU.mult)\
                    .then_inc(s["c_ln1"], 1)
                dve.wait_ge(s["c_ln1"], 2 * g + 2)
                wait(dve, "xT_ps", g)
                for i in range(2):
                    ins = dve.tensor_scalar(xn[:, i, :], xin[:, i, :], mv1[:, i, 0:1], rs1[:, 2, i:i + 1],
                                            ALU.subtract, ALU.mult)
                ins.then_inc(s["xn_ready"], 1)

            def x_plus_bo(g, p):
                dve.tensor_tensor(xb[:, p, :, :], xin[:, :, :],
                                  bob[:, :].unsqueeze(1).to_broadcast([P, 2, D]), ALU.add)\
                    .then_inc(s["xb_ready"], 1)

            def k2(v):
                return v.rearrange("p (k n) -> p k n", k=KT)

            ln_1(0, 0)
            for n in range(4):
                dve.wait_ge(s["wT_hi"], n + 1)
                dve.tensor_tensor(wal[:, n, :, :], k2(banks[n][:, :]), wah[:, n, :, :], ALU.subtract)\
                    .then_inc(s["wT_lo"], 1)
            dve.wait_ge(s["bc_ready"], 1)
            bcol_q, bcol_k = bcols[:, 64:66], bcols[:, 66:68]
            link(dve.tensor_tensor(tbq[:, :, :], bcol_q.unsqueeze(2).to_broadcast([P, KT, B]),
                                   tau4[:, :].unsqueeze(1).to_broadcast([P, KT, B]), ALU.mult))

            def turned_lo(g):
                for n, ps, ready, done in ((0, pA, "xh_ready", "xl_ready"), (2, pB, "ch_ready", "cl_ready")):
                    dve.wait_ge(s[ready], g + 1)
                    dve.tensor_tensor(xT[:, n + 1, :, :], k2(ps[:, :]), xT[:, n, :, :], ALU.subtract)\
                        .then_inc(s[done], 1)

            def qk_parts(g):
                dve.wait_ge(s["q_ps"], g + 1)
                dve.tensor_tensor(qk32[:, :, :].rearrange("p k (b n) -> p k b n", b=2),
                                  pA[:, :].rearrange("p (k b n) -> p k b n", k=KT, b=2),
                                  tbq[:, :, bass.ds(g * 2, 2)].unsqueeze(3).to_broadcast([P, KT, 2, S]),
                                  ALU.add).then_inc(s["q32_ready"], 1)
                dve.wait_ge(s["qh_ready"], g + 1)
                dve.tensor_tensor(qkc[:, 1, :, :], qk32[:, :, :], qkc[:, 0, :, :], ALU.subtract)\
                    .then_inc(s["ql_ready"], 1)
                dve.wait_ge(s["k_ps"], g + 1)
                dve.wait_ge(s["ql_ready"], g + 1)
                dve.tensor_tensor(qk32[:, :, :], k2(pB[:, :]),
                                  bcol_k.unsqueeze(2).to_broadcast([P, KT, 2 * S]), ALU.add)\
                    .then_inc(s["k32_ready"], 1)
                dve.wait_ge(s["kh_ready"], g + 1)
                dve.tensor_tensor(qkc[:, 3, :, :], qk32[:, :, :], qkc[:, 2, :, :], ALU.subtract)\
                    .then_inc(s["kl_ready"], 1)

            def v_out(g, p):
                dve.wait_ge(s["v_ps"], g + 1)
                wait(dve, "po_ps", 2 * (g - 1))
                dve.tensor_tensor(V_[:, p, :, :, 0:DK],
                                  pA[:, :].rearrange("p (b h d) -> p b h d", b=2, d=DK),
                                  bvb[:, :].rearrange("p (h d) -> p h d", d=DK).unsqueeze(1)
                                  .to_broadcast([P, 2, H, DK]), ALU.add).then_inc(s["v_ready"], 1)

            def maxima(b):
                for u in range(4):
                    dve.wait_ge(s["s_ps"], 4 * b + u + 1)
                    dve.reduce_max(mx[:, unit_heads(u)], psS[u % 2][:, :].rearrange("p (h n) -> p h n", h=4),
                                   AX.X).then_inc(s["m_red"], 1)
                dve.wait_ge(s["m_red"], 4 * b + 4)
                wait(dve, "mT_ps", b)
                dve.tensor_scalar(mm[:, 0:H], mx[:, :], -1.0, None, ALU.mult).then_inc(s["c_mm"], 1)
                dve.wait_ge(s["c_mm"], b + 1)
                dve.scalar_tensor_tensor(out=mm[:, H:2 * H], in0=mx[:, :], scalar=-1.0, in1=mm[:, 0:H],
                                         op0=ALU.mult, op1=ALU.subtract).then_inc(s["mm_ready"], 1)

            def heads_out(b):
                dve.wait_ge(s["po_ps"], b + 1)
                dve.reciprocal(rec[:, :], pO[:, :, DK]).then_inc(s["c_on"], 1)
                dve.wait_ge(s["c_on"], b + 1)
                wait(dve, "oT_ps", b)
                dve.tensor_tensor(on[:, :, :], pO[:, :, 0:DK], rec[:, :].unsqueeze(2).to_broadcast([P, H, DK]),
                                  ALU.mult).then_inc(s["on_ready"], 1)

            def oT_lo(b):
                dve.wait_ge(s["oh_ready"], b + 1)
                dve.tensor_tensor(oT[:, 1, :, :], pT6, oT[:, 0, :, :], ALU.subtract).then_inc(s["ol_ready"], 1)

            def residual(b, bb, p):
                dve.wait_ge(s["y_ps"], b + 1)
                wait(dve, x1_stored[bb], 8 * (b - bb))
                dve.tensor_tensor(x1[:, bb, :], pY6, xb[:, p, bb, :], ALU.add).then_inc(s["x1_ready"], 1)
                dve.wait_ge(s["x1_ready"], b + 1)
                dve.bn_stats(st2[:, :], x1[:, bb, :]).then_inc(s["c_ln2"], 1)
                own_wait(dve, "c_ln2", b + 1)
                dve.bn_aggr(mv2[:, :], st2[:, :]).then_inc(s["ln2_stats"], 1)
                dve.wait_ge(s["rstd2"], b + 1)
                wait(dve, xn2_stored[bb], 8 * (b - bb))
                dve.tensor_scalar(xn2[:, bb, :], x1[:, bb, :], mv2[:, 0:1], rs2[:, 1:2],
                                  ALU.subtract, ALU.mult).then_inc(s["xn2_ready"], 1)

            def score(b):
                dve.wait_ge(s["r_ps"], b + 1)
                dve.tensor_tensor(sc[:, :, bass.ds(b, 1)], pR.unsqueeze(2), brb[:, :].unsqueeze(2), ALU.add)\
                    .then_inc(s["sc_ready"], 1)

            def step(t, p):
                wait(dve, "xb_ready", t if not known(t) else min(t, G))
                for bb in range(2):
                    b = 2 * t - 2 + bb
                    prev = has(t, 2 - bb, G + 1)
                    if has(t, 1, G + 1):
                        maxima(b)
                    if prev:
                        oT_lo(b - 1)
                    if has(t, 0, G):
                        if bb == 0:
                            turned_lo(t)
                        else:
                            v_out(t, p)
                    if prev:
                        residual(b - 1, 1 - bb, p if bb == 0 else 1 - p)
                    if bb == 0 and has(t, 0, G):
                        x_plus_bo(t, p)
                        qk_parts(t)
                    if bb == 1 and has(t, 0, G - 1):
                        ln_1(t + 1, 1 - p)
                    if prev:
                        score(b - 1)
                    if has(t, 1, G + 1):
                        heads_out(b)

            attention_steps(dve, step)
            oT_lo(B - 1)
            residual(B - 1, 1, 1)
            score(B - 1)
            dve.wait_ge(s["sc_ready"], B)
            dve.wait_ge(s["const_ready"], 1)

            link = chain(dve, "c_route")

            def over_experts(v):
                return v.rearrange("p e b -> p b e")

            def per_batch(v):
                return v.unsqueeze(1).to_broadcast([P, E, B])

            scores = sc[:, :, :]
            for k in range(2):
                best, first = rb[:, k, :], rb[:, 2 + k, :]
                link(dve.reduce_max(best, over_experts(scores), AX.X))
                link(dve.tensor_tensor(ra[:, 0, :, :], scores, per_batch(best), ALU.is_equal))
                link(dve.tensor_tensor(ra[:, 0, :, :], ra[:, 0, :, :], rev[:, :].unsqueeze(2).to_broadcast([P, E, B]),
                                       ALU.mult))
                link(dve.reduce_max(first, over_experts(ra[:, 0, :, :]), AX.X))
                link(dve.tensor_tensor(hot[:, k, :, :], ra[:, 0, :, :], per_batch(first), ALU.is_equal))
                if k == 0:
                    link(dve.scalar_tensor_tensor(out=ra[:, 1, :, :], in0=hot[:, 0, :, :], scalar=-3.0e38,
                                                  in1=scores, op0=ALU.mult, op1=ALU.add))
                    scores = ra[:, 1, :, :]
            dve.tensor_tensor(rb[:, 4, :], rb[:, 1, :], rb[:, 0, :], ALU.subtract).then_inc(s["gap_ready"], 1)
            mask3 = mask[:, :].rearrange("p (e b) -> p e b", e=E)
            dve.tensor_tensor(mask3, hot[:, 0, :, :], hot[:, 1, :, :], ALU.add).then_inc(s["mask_ready"], 1)
            dve.wait_ge(s["e_ready"], 1)
            link(dve.tensor_scalar(rb[:, 6, :], rb[:, 5, :], 1.0, None, ALU.add))
            pw = rb[:, 6:8, :]
            link(dve.reciprocal(rb[:, 6, :], rb[:, 6, :]))
            link(dve.tensor_tensor(rb[:, 7, :], rb[:, 5, :], rb[:, 6, :], ALU.mult))
            link(dve.tensor_copy(vals[:, 1, :].rearrange("p (c b) -> p c b", c=2), pw))
            dve.tensor_copy(vals[:, 0, :].rearrange("p (c b) -> p c b", c=2), tokval[:, :, :])
            link(dve.tensor_tensor(vals[:, 2, :].rearrange("p (c b) -> p c b", c=2), pw,
                                   vals[:, 1, :].rearrange("p (c b) -> p c b", c=2), ALU.subtract))
            ranks, counts = pA[:, 0:P], pA[:, P:2 * P]
            flat = [ra[:, i, :, :].rearrange("p e b -> p (e b)") for i in range(3)]
            dve.wait_ge(s["rank_ps"], 1)
            link(dve.tensor_tensor_scan(flat[0], notfirst[:, :], counts, 0.0, ALU.mult, ALU.add))
            link(dve.tensor_tensor(ra[:, 1, :, :], ra[:, 0, :, B - 1:B].to_broadcast([P, E, B]),
                                   steps128[:, :].unsqueeze(1).to_broadcast([P, E, B]), ALU.is_gt))
            link(dve.reduce_sum(rc[:, 0, :], ra[:, 1, :, :], AX.X))
            link(dve.tensor_tensor_scan(rc[:, 1, :], onesh[:, 0:E], rc[:, 0, :], 0.0, ALU.mult, ALU.add))
            link(dve.tensor_tensor(rc[:, 2, :], rc[:, 1, :], rc[:, 0, :], ALU.subtract))
            link(dve.tensor_tensor(flat[0], flat[0], counts, ALU.subtract))
            link(dve.tensor_tensor(flat[0], flat[0], ranks, ALU.add))
            link(dve.scalar_tensor_tensor(out=ra[:, 2, :, :], in0=rc[:, 2, :].unsqueeze(2).to_broadcast([P, E, B]),
                                          scalar=float(P), in1=ra[:, 0, :, :], op0=ALU.mult, op1=ALU.add))
            for k in range(2):
                link(dve.tensor_tensor(ra[:, k, :, :], hot[:, k, :, :], ra[:, 2, :, :], ALU.mult))
                link(dve.reduce_sum(pos[:, k, :], over_experts(ra[:, k, :, :]), AX.X))
            link(dve.tensor_copy(posi[:, 0, :], pos[:, :, :].rearrange("p c b -> p (c b)")))
            link(dve.tensor_scalar(posi[:, 1, :], posi[:, 0, :], 7, None, ALU.arith_shift_right))
            link(dve.tensor_scalar(posi[:, 2, :], posi[:, 0, :], P - 1, None, ALU.bitwise_and))
            link(dve.tensor_copy(posf[:, :, :], posi[:, 1:3, :]))
            link(dve.tensor_tensor(hot_tile, tile_no[:, :].unsqueeze(1).to_broadcast([P, 2 * B, NT]),
                                   posf[:, 0, :].unsqueeze(2).to_broadcast([P, 2 * B, NT]), ALU.is_equal))
            for v in range(3):
                dve.tensor_tensor(hot_val[:, :, v, :], hot_tile,
                                  vals[:, v, :].unsqueeze(2).to_broadcast([P, 2 * B, NT]), ALU.mult)
            dve.tensor_tensor(hot_slot, slot_no[:, :].unsqueeze(1).to_broadcast([P, 2 * B, P]),
                              posf[:, 1, :].unsqueeze(2).to_broadcast([P, 2 * B, P]), ALU.is_equal)\
                .then_inc(s["hot_ready"], 1)
            link(dve.tensor_tensor(tile_e, rc[0:1, 1, :].unsqueeze(1).to_broadcast([1, NT, E]),
                                   tile_no[0:1, :].unsqueeze(2).to_broadcast([1, NT, E]), ALU.is_le))
            link(dve.reduce_sum(tile_f[:, 0, :], tile_e, AX.X))
            link(dve.tensor_scalar(tile_exp[:, :], tile_f[:, 0, :], float(E - 1), None, ALU.min))
            dve.wait_ge(s["slot_ps"], 1)
            link(dve.tensor_copy(slot_t[:, :, :], pB[:, 0:2 * NT].rearrange("p (a j) -> p a j", a=2)))
            link(dve.tensor_tensor(slot_w[:, :], slot_t[:, 1, :], pB[:, 2 * NT:3 * NT], ALU.add))
            link(dve.tensor_scalar(slot_t[:, 1, :], slot_t[:, 0, :], 0.0, part_no[:, 0:1], ALU.is_equal, ALU.mult))
            dve.scalar_tensor_tensor(out=slot_rows[:, :], in0=slot_t[:, 0, :], scalar=float(T),
                                     in1=slot_t[:, 1, :], op0=ALU.add, op1=ALU.add).then_inc(s["routed"], 1)

            def step(t, p):
                if has(t, 0, NT):
                    dve.wait_ge(s["gh_ready"], t + 1)
                    dve.tensor_tensor(xT[:, 2 * p + 1, :, 0:P], k2((pA, pB)[p][:, 0:KT * P]),
                                      xT[:, 2 * p, :, 0:P], ALU.subtract).then_inc(s["gl_ready"], 1)
                if has(t, 1, NT + 1):
                    j, q = t - 1, 1 - p
                    dve.wait_ge(s["gelu_done"], j + 1)
                    wait(dve, "yy_ps", j - 1)
                    h32 = hid[q].rearrange("p c n -> p (c n)")
                    dve.tensor_copy(hh[q], h32).then_inc(s["hh_done"], 1)
                    dve.wait_ge(s["hh_done"], j + 1)
                    dve.tensor_tensor(hl[q], h32, hh[q], ALU.subtract).then_inc(s["hl_done"], 1)
                if has(t, 2, NT + 2):
                    j = t - 2
                    dve.wait_ge(s["yy_ps"], j + 1)
                    wait(dve, "added", 16 * (j - 1))
                    dve.tensor_scalar(yw[:, p, :], banks[6 + p][:, 0:D], slot_w[:, bass.ds(j, 1)], None,
                                      ALU.mult).then_inc(s["yy_ready"], 1)

            expert_steps(dve, step)

        @block.tensor
        def _(pe):
            def split_product(ps, lhs, rhs, first=True, last=True):
                for k in range(KT):
                    for i, (a, b_) in enumerate(((0, 0), (0, 1), (1, 0))):
                        ins = pe.matmul(ps, lhs(a, k), rhs(b_, k), start=first and k == 0 and i == 0,
                                        stop=last and k == KT - 1 and i == 2)
                return ins

            wa = (wah, wal)
            pe.wait_ge(s["const_ready"], 1)
            pe.wait_ge(s["wa_loaded"], 64)
            for n in range(4):
                for k in range(KT):
                    for a in range(2):
                        ins = pe.transpose(banks[n][:, k * D + a * P:k * D + (a + 1) * P],
                                           stage[:, n // 2, (n % 2) * 512 + a * D + k * P:(n % 2) * 512 + a * D + (k + 1) * P], ident[:, :])
                ins.then_inc(s["wT_ps"], 1)
            pe.wait_ge(s["bcols_loaded"], 48)
            pe.transpose(pA[:, 0:68], bias_rows[0:68, :], ident[0:68, 0:68]).then_inc(s["bc_ps"], 1)

            def turn(g, p):
                pe.wait_ge(s["xn_ready"], g + 1)
                wait(pe, "v_ready", g)
                if known(g) and g == 0:
                    pe.wait_ge(s["bc_ready"], 1)
                for k in range(KT):
                    for i in range(2):
                        ins = pe.transpose(pA[:, (2 * k + i) * P:(2 * k + i + 1) * P],
                                           xn[:, i, k * P:(k + 1) * P], ident[:, :])
                ins.then_inc(s["xT_ps"], 1)
                pe.wait_ge(c_loaded, 16 * (g + 1))
                wait(pe, "k32_ready", g)
                for k in range(KT):
                    for i in range(2):
                        ins = pe.transpose(pB[:, (2 * k + i) * P:(2 * k + i + 1) * P],
                                           cin[:, i, k * P:(k + 1) * P], ident[:, :])
                ins.then_inc(s["cT_ps"], 1)

            def project_qk(g):
                for n, ps, ready, done in ((0, pA, "xl_ready", "q_ps"), (1, pB, "cl_ready", "k_ps")):
                    pe.wait_ge(s[ready], g + 1)
                    for c in range(KT):
                        ins = split_product(ps[:, c * 2 * S:(c + 1) * 2 * S],
                                            lambda a, k: wa[a][:, n, k, c * P:(c + 1) * P],
                                            lambda a, k: xT[:, 2 * n + a, k, :])
                    ins.then_inc(s[done], 1)

            def project_v(g):
                pe.wait_ge(s["q32_ready"], g + 1)
                for i in range(2):
                    ins = split_product(pA[:, i * D:(i + 1) * D],
                                        lambda a, k: xT[:, 2 + a, k, i * S:(i + 1) * S],
                                        lambda a, k: wa[a][:, 2, k, :])
                ins.then_inc(s["v_ps"], 1)

            def scores(b, bb, p, keys_first):
                for u in range(4):
                    r = 64 * (u % 2)
                    ps = (psST if keys_first else psS)[u % 2]
                    wait(pe, "exp_done" if keys_first else "m_red", 4 * b + u - 1)
                    for i in range(4):
                        j = 4 * (u // 2) + i
                        q = QS[r:r + ROWS, p, j, bb * S:(bb + 1) * S]
                        k = KS[r:r + ROWS, p, j, bb * S:(bb + 1) * S]
                        o = ps[:, i * S:(i + 1) * S]
                        if keys_first:
                            pe.matmul(o, k, q, start=True, stop=False)
                            ins = pe.matmul(o, sel[:, 2 * j + u % 2:2 * j + u % 2 + 1].to_broadcast([2 * H, S]), mT[:, :], start=False, stop=True)
                        else:
                            ins = pe.matmul(o, q, k, start=True, stop=True)
                    ins.then_inc(s["st_ps" if keys_first else "s_ps"], 1)

            def values(b, bb, p):
                pe.wait_ge(s["exp_done"], 4 * b + 4)
                wait(pe, "on_ready", b)
                for h in range(H):
                    ins = pe.matmul(pO[:, h, :], PT[:, h, :], V[:, p, bb, h, :], start=True, stop=True)
                ins.then_inc(s["po_ps"], 1)

            def turn_heads(b):
                pe.wait_ge(s["on_ready"], b + 1)
                wait(pe, "sc_ready", b)
                for k in range(KT):
                    ins = pe.transpose(pT6[:, k, :], on[:, :, :].rearrange("p h d -> p (h d)")[:, k * P:(k + 1) * P],
                                       ident[:, :])
                ins.then_inc(s["oT_ps"], 1)

            def out_product(b):
                pe.wait_ge(s["ol_ready"], b + 1)
                wait(pe, "x1_ready", b)
                split_product(pY6, lambda a, k: oT[:, a, k, :], lambda a, k: wa[a][:, 3, k, :])\
                    .then_inc(s["y_ps"], 1)

            def turn_xn2(b, bb):
                pe.wait_ge(s["xn2_ready"], b + 1)
                for k in range(KT):
                    ins = pe.transpose(pT6[:, k, :], xn2[:, bb, k * P:(k + 1) * P], ident[:, :])
                ins.then_inc(s["x2T_ps"], 1)

            def route(b):
                pe.wait_ge(s["x2T_ready"], b + 1)
                for k in range(KT):
                    ins = pe.matmul(pR, xn2T[:, k, :], wr[:, k, :], start=(k == 0), stop=(k == KT - 1))
                ins.then_inc(s["r_ps"], 1)

            pe.wait_ge(s["small_in"], 16 * 7)
            pe.wait_ge(s["wT_lo"], 4)

            def step(t, p):
                for bb in range(2):
                    b = 2 * t - 2 + bb
                    att = has(t, 1, G + 1)
                    prev = has(t, 2 - bb, G + 1)
                    if att:
                        if bb == 0:
                            pe.wait_ge(stack_ready[1 - p], 14 * 8 * (t - 1 - (1 - p)) + 14 * 16)
                        scores(b, bb, 1 - p, False)
                    if prev:
                        turn_heads(b - 1)
                    if has(t, 0, G):
                        if bb == 0:
                            turn(t, p)
                        else:
                            project_v(t)
                    if prev:
                        out_product(b - 1)
                    if att:
                        pe.wait_ge(s["mm_ready"], b + 1)
                        wait(pe, "mT_ready", b)
                        pe.transpose(pM[0:2 * H, :], mm[:, :], identh[:, :]).then_inc(s["mT_ps"], 1)
                        pe.wait_ge(s["mT_ready"], b + 1)
                        scores(b, bb, 1 - p, True)
                    if prev:
                        turn_xn2(b - 1, 1 - bb)
                    if bb == 0 and has(t, 0, G):
                        project_qk(t)
                    if prev:
                        route(b - 1)
                    if att:
                        if bb == 0:
                            pe.wait_ge(s["v_ready"], t)
                        values(b, bb, 1 - p)

            attention_steps(pe, step)
            turn_heads(B - 1)
            out_product(B - 1)
            turn_xn2(B - 1, 1)
            route(B - 1)

            pe.wait_ge(s["mask_ready"], 1)
            pe.matmul(pA[:, 0:P], trih[:, :], mask[:, :], start=True, stop=True)
            pe.matmul(pA[:, P:2 * P], onesh[:, :], mask[:, :], start=True, stop=True).then_inc(s["rank_ps"], 1)
            pe.wait_ge(s["hot_ready"], 1)
            for i in range(2 * B):
                ins = pe.matmul(pB[:, 0:3 * NT], hot_slot[:, i, :],
                                hot_val[:, i, :, :].rearrange("p v j -> p (v j)"),
                                start=(i == 0), stop=(i == 2 * B - 1))
            ins.then_inc(s["slot_ps"], 1)
            pe.wait_ge(s["w_lo"], 4 * E)
            pe.wait_ge(s["b2_moved"], 16)
            pe.wait_ge(s["routed"], 1)

            def step(t, p):
                if has(t, 0, NT):
                    pe.wait_ge(rows_in[p], 8 * (t - p) + 16)
                    wait(pe, "gl_ready", t - 1)
                    for k in range(KT):
                        ins = pe.transpose((pA, pB)[p][:, k * P:(k + 1) * P], xs[:, p, k * P:(k + 1) * P],
                                           ident[:, :])
                    ins.then_inc(s["gT_ps"], 1)
                if has(t, 1, NT + 1):
                    j, q = t - 1, 1 - p
                    e = pe.value_load(tile_exp[0:1, bass.ds(j, 1)], min_val=0, max_val=E - 1)
                    pe.wait_ge(s["gl_ready"], j + 1)
                    wait(pe, "gelu_done", j - 1)
                    for c in range(FC):
                        ins = split_product(banks[2 * q + c // 4][:, (c % 4) * P:(c % 4 + 1) * P],
                                      lambda a, k: (w1h, w1l)[a][:, bass.ds(e * (KT * F) + k * F + c * P, P)],
                                      lambda a, k: xT[:, 2 * q + a, k, 0:P])
                        if c % 4 == 3:
                            ins.then_inc(s["h_ps"], 1)
                if has(t, 2, NT + 2):
                    j = t - 2
                    e = pe.value_load(tile_exp[0:1, bass.ds(j, 1)], min_val=0, max_val=E - 1)
                    ps = banks[6 + p][:, 0:D]
                    pe.wait_ge(s["hl_done"], j + 1)
                    wait(pe, "yy_ready", j - 1)
                    pe.matmul(ps, onesh[0:2, :], b2r[:, bass.ds(e * D, D)], start=True, stop=False)
                    for c in range(FC):
                        for a, b_ in ((0, 0), (0, 1), (1, 0)):
                            ins = pe.matmul(ps, (hh, hl)[a][p][:, c * P:(c + 1) * P],
                                            (w2h, w2l)[b_][:, bass.ds(e * (FC * D) + c * D, D)],
                                            start=False, stop=(c == FC - 1 and a == 1))
                    ins.then_inc(s["yy_ps"], 1)

            expert_steps(pe, step)


_INS = ['x', 'ctx_1024', 'condB_tau', 'fside_BxS2_0', 'L0_xcond_Wq', 'L0_xcond_bq', 'L0_xcond_Wk', 'L0_xcond_bk',
        'L0_xcond_Wv', 'L0_xcond_bv', 'L0_xcond_Wo', 'L0_xcond_bo', 'L0_ffn_W1', 'L0_ffn_b1', 'L0_ffn_W2',
        'L0_ffn_b2', 'L0_ffn_Wr', 'L0_ffn_br']


def kernel(**inputs):
    import numpy as _np
    import concourse.bacc as _bacc
    from concourse import mybir as _mybir
    from concourse.bass_utils import run_bass_kernel_spmd as _run

    nc = _bacc.Bacc("TRN2", target_bir_lowering=False, num_devices=1)
    arrays, args = {}, []
    for name in _INS:
        a = _np.ascontiguousarray(inputs[name])
        arrays[f"in_{name}_dram"] = a
        args.append(nc.dram_tensor(f"in_{name}_dram", a.shape, _mybir.dt.from_np(a.dtype), kind="ExternalInput").ap())
    args.append(nc.dram_tensor("out_dram", (T + P, D), _mybir.dt.float32, kind="ExternalOutput").ap())
    moe_block_kernel(nc, *args)
    r = _run(nc, [arrays], core_ids=[0])
    return r.results[0]["out_dram"][0:T].reshape(B, S, D)
```

```python
import concourse.bass as bass
from concourse import mybir
from contextlib import ExitStack

P = 128
B, S, D = 16, 128, 256
KT = D // P
H, DK = 16, 16
E, F = 8, 1024
FC = F // P
T = B * S
G = B // 2
SMALL = 10
TW = 2 * P
NT = (2 * T - E) // TW + E
NS = 2 * NT
EPS = 1e-5

fp32 = mybir.dt.float32
fp16 = mybir.dt.float16
i32 = mybir.dt.int32
ALU = mybir.AluOpType
ACT = mybir.ActivationFunctionType
AX = mybir.AxisListType


def known(t):
    return isinstance(t, int)


def moe_block_kernel(nc, x, ctx_in, tau, side, Wq, bq, Wk, bk, Wv, bv, Wo, bo,
                     W1, b1, W2, b2, Wr, br, out):
    stack = ExitStack()
    with stack:
        def sb(name, shape, dt=fp32):
            return stack.enter_context(nc.sbuf_tensor(name, shape, dt))

        def sem(name):
            return stack.enter_context(nc.semaphore(name))

        q_dram = nc.dram_tensor("q_dram", (2, H // 4, 2, 3, DK, 4 * S), fp16, kind="Internal").ap()
        k_dram = nc.dram_tensor("k_dram", (2, H // 4, 2, 3, DK, 4 * S), fp16, kind="Internal").ap()
        delta_dram = nc.dram_tensor("delta_dram", (2, B, S), fp16, kind="Internal").ap()
        rows_dram = nc.dram_tensor("rows_dram", (2, E + 4, D), fp16, kind="Internal").ap()
        xn2_dram = nc.dram_tensor("xn2_dram", (T + P, D), fp32, kind="Internal").ap()

        w1h = sb("w1h", [P, E * KT * F], fp16)
        w1l = sb("w1l", [P, E * KT * F], fp16)
        w2h = sb("w2h", [P, E * FC * D], fp16)
        w2l = sb("w2l", [P, E * FC * D], fp16)
        stage = sb("stage", [P, 2, 1024])
        wah = sb("wah", [P, 4, KT, D], fp16)
        wal = sb("wal", [P, 4, KT, D], fp16)
        wr = sb("wr", [P, KT, E])
        brb = sb("brb", [P, E])
        bob = sb("bob", [P, D])
        bcols = sb("bcols", [P, E * FC])
        tau4 = sb("tau4", [P, B])
        qrow = sb("qrow", [3, D], fp16)
        trow = sb("trow", [3, B], fp16)
        kvrow = sb("kvrow", [2, 2, D], fp16)
        ident = sb("ident", [P, P])
        identh = sb("identh", [P, P], fp16)
        onesh = sb("onesh", [P, P], fp16)
        trih = sb("trih", [P, P], fp16)
        sel = sb("sel", [2 * H, H], fp16)
        nhalf = sb("nhalf", [P, 2])
        rev = sb("rev", [P, E])
        steps = sb("steps", [P, B])
        notfirst = sb("notfirst", [P, E * B], fp16)
        tokval = sb("tokval", [P, 2, B], fp16)
        slot_no = sb("slot_no", [P, P], fp16)
        tile_no = sb("tile_no", [P, NS], fp16)
        part_no = sb("part_no", [P, 1])
        xin = sb("xin", [P, 2, D])
        cin = sb("cin", [P, 2, D])
        xn = sb("xn", [P, 2, D])
        xb = sb("xb", [P, 2, 2, D])
        st1 = sb("st1", [P, 2, 6])
        mv1 = sb("mv1", [P, 2, 2])
        rs1 = sb("rs1", [P, 3, 2])
        xT = sb("xT", [P, 4, KT, 2 * S], fp16)
        qkc = sb("qkc", [P, 4, KT, 2 * S], fp16)
        QK = sb("QK", [P, 2, 2, H // 2, 2 * S], fp16)
        V = sb("V", [P, 2, 2, 2, H, DK + 1], fp16)
        PT = sb("PT", [P, 3 * 1024])
        mx = sb("mx", [P, H])
        mm = sb("mm", [P, 2 * H], fp16)
        mT = sb("mT", [2 * H, S], fp16)
        rec = sb("rec", [P, H])
        on = sb("on", [P, H, DK])
        oT = sb("oT", [P, 2, KT, S], fp16)
        x1 = sb("x1", [P, 2, D])
        xn2 = sb("xn2", [P, 2, D])
        st2 = sb("st2", [P, 6])
        mv2 = sb("mv2", [P, 2])
        rs2 = sb("rs2", [P, 2])
        xn2T = sb("xn2T", [P, KT, S])
        sc = sb("sc", [P, E, B])
        rc = sb("rc", [P, 3, E])
        slot_rows = sb("slot_rows", [P, NS], i32)

        QS, KS = QK[:, 0, :, :, :], QK[:, 1, :, :, :]
        flatPT = PT[:, :]
        bias_rows = flatPT[:, 0:P]
        rows32 = flatPT[0:E + 4, 128:384]
        delta = flatPT[0:B, 384:512]
        rparts = flatPT[0:E + 4, 512:768].bitcast(fp16).rearrange("p (r d) -> p r d", r=2)
        dparts = flatPT[0:B, 768:896].bitcast(fp16).rearrange("p (r s) -> p r s", r=2)
        P32 = PT[:, 0:1024].rearrange("p (a n) -> p a n", a=2)
        PH, PL = [PT[:, r * 1024:(r + 1) * 1024].bitcast(fp16).rearrange("p (h n) -> p h n", n=S) for r in (1, 2)]
        flatxb = xb[:, :, :, :].rearrange("p a b d -> p (a b d)")
        hot = flatxb[:, 0:256].rearrange("p (c e b) -> p c e b", c=2, e=E)
        ra = flatxb[:, 256:640].rearrange("p (c e b) -> p c e b", c=3, e=E)
        rb = flatxb[:, 640:768].rearrange("p (c b) -> p c b", b=B)
        tile_e = xn[0:1, :, :].rearrange("p a d -> p (a d)")[:, 0:NT * E].rearrange("p (j e) -> p j e", e=E)
        flatQK = QK[:, :, :, :, :].rearrange("p q a b c -> p (q a b c)")
        hot_tile = flatQK[:, 0:2 * B * NS].rearrange("p (i j) -> p i j", j=NS)
        b2r = V[0:2, :, :, :, :, :].rearrange("p r a b h d -> p (r a b h d)")[:, 0:E * D]
        hot_slot = flatPT[:, 0:2048].bitcast(fp16)\
            .rearrange("p (i r) -> p i r", r=P)
        hot_val = flatQK[:, 2 * B * NS:2 * B * 4 * NS].rearrange("p (i v j) -> p i v j", v=3, j=NS)
        flatqk = qkc[:, :, :, :].rearrange("p a k n -> p (a k n)")
        mask = flatqk[:, 0:128]
        pos = flatqk[:, 128:192].bitcast(fp32).rearrange("p (c b) -> p c b", c=2)
        posi = flatqk[:, 192:384].bitcast(i32).rearrange("p (c b) -> p c b", c=3)
        posf = flatqk[:, 384:448].rearrange("p (c b) -> p c b", c=2)
        vals = flatqk[:, 448:544].rearrange("p (c b) -> p c b", c=3)
        slot_t = flatqk[:, 544:544 + 4 * NS].bitcast(fp32).rearrange("p (c j) -> p c j", c=2)
        slot_w = flatqk[:, 896:896 + 2 * NS].bitcast(fp32)
        tile_f = flatqk[0:1, 768:768 + 2 * NT].bitcast(fp32)
        tile_exp = qrow[0:1, 0:2 * NT].bitcast(i32)
        idxg, idxs = wr[:, 0, 0:4].bitcast(i32), wr[:, 0, 4:6].bitcast(i32)
        xs = (xin, cin)
        hid = [PT[:, u * 512:(u + 1) * 512] for u in range(4)]
        hh, hl = [[flatQK[:, (2 * a + r) * 2048:(2 * a + r + 1) * 2048].rearrange("p (c n) -> p c n", n=TW)
                   for r in range(2)] for a in range(2)]
        yw = (x1, xn2)

        banks = [stack.enter_context(nc.psum_tensor(f"bank{i}", [P, 512], fp32)) for i in range(8)]
        psS, psST, pA, pB = banks[0:2], banks[2:4], banks[4], banks[5]
        pT6 = banks[6][:, 0:256].rearrange("p (k n) -> p k n", k=KT)
        pY6 = banks[6][:, 256:512]
        pO = banks[7][:, 0:H * (DK + 1)].rearrange("p (h d) -> p h d", d=DK + 1)
        pM = banks[7][:, 288:352].bitcast(fp16)
        pR = pY6[:, 0:E]

        names = """zeroed const_ready ones_ready bcols_loaded wa_loaded small_in
            wT_ps wT_hi wT_lo bc_ps bc_ready delta_split delta_stored rows_split rows_stored rows_in
            tau_ready b2_moved zeros_stored w_hi w_lo
            ln1_stats rstd1 xb_ready xn_ready xT_ps cT_ps xh_ready ch_ready xl_ready cl_ready q_ps k_ps
            qh_ready kh_ready ql_ready kl_ready v_ps vh_ready vl_ready q_stored k_stored
            s_ps m_red mm_ready mT_ps mT_ready st_ps exp_done pl_even pl_odd po_ps on_ready oT_ps oh_ready ol_ready
            y_ps x1_ready ln2_stats rstd2 xn2_ready x2T_ps x2T_ready r_ps sc_ready
            c_setup c_pool c_ln1 c_rs1 c_mm c_on c_ln2 c_rs2 c_route
            mask_ready gap_ready e_ready rank_ps hot_ready slot_ps routed
            idxg_ready idxs_ready gT_ps gh_ready gl_ready h_ps gelu_done hh_done hl_done yy_ps yy_ready
            added""".split()
        s = {n: sem(n) for n in names}
        x_loaded, c_loaded = sem("x_loaded"), sem("c_loaded")
        stack_ready = [sem(f"stack_ready{i}") for i in range(2)]
        x1_stored = [sem(f"x1_stored{i}") for i in range(2)]
        xn2_stored = [sem(f"xn2_stored{i}") for i in range(2)]
        w_loaded = [sem(f"w_loaded{i}") for i in range(2)]
        rows_in = [sem(f"rows_in{i}") for i in range(2)]
        block = stack.enter_context(nc.Block())

        def wait(eng, name, n):
            if not known(n) or n > 0:
                eng.wait_ge(s[name] if isinstance(name, str) else name, n)

        def own_wait(eng, name, n):
            if known(n):
                eng.wait_ge(s[name], n)
            else:
                n = eng.to_reg(n)
                eng.wait_ge(s["const_ready"], 1)
                eng.wait_ge(s[name], n)

        def chain(eng, name, base=0):
            k = [0]

            def link(ins):
                k[0] += 1
                ins.then_inc(s[name], 1)
                eng.wait_ge(s[name], base + k[0])
            return link

        def attention_steps(eng, step):
            for t in range(3):
                step(t, t % 2)
            with eng.Fori(1, 3) as i:
                step(i * 2 + 1, 1)
                step(i * 2 + 2, 0)
            for t in range(G - 1, G + 2):
                step(t, t % 2)

        def batch_in(t, bb, late):
            return not known(t) or 0 <= 2 * t - 2 + bb - late < B

        def expert_steps(eng, step):
            for t in range(4):
                step(t, t % 2)
            with eng.Fori(2, (NT - 2) // 2) as i:
                step(i * 2, 0)
                step(i * 2 + 1, 1)
            for t in range((NT - 2) // 2 * 2, NT + 2):
                step(t, t % 2)

        def has(t, lo, hi):
            return not known(t) or lo <= t < hi

        ROWS = 3 * DK + 2

        def head_of(place):
            u, j = place // 4, 4 * (place // 8) + place % 4
            return 8 * (j % 2) + 2 * (j // 2) + u % 2

        @block.sync
        def _(sp):
            def load_x(g):
                wait(sp, "xn_ready", g)
                own_wait(sp, "xb_ready", g)
                sp.dma_start(xin[:, :, :], x[bass.ds(g * 2, 2), :, :].rearrange("b s d -> s b d"))\
                  .then_inc(x_loaded, 16)

            def load_ctx(g):
                own_wait(sp, "cT_ps", g)
                sp.dma_start(cin[:, :, :], ctx_in[bass.ds(g * 2, 2), :, :].rearrange("b s d -> s b d"))\
                  .then_inc(c_loaded, 16)

            def load_w(e, n):
                wait(sp, "w_lo", 4 * e + n - 1)
                if n < 2:
                    src = W1[bass.ds(e, 1), n * P:(n + 1) * P, :].rearrange("e p n -> p (e n)")
                    dst = stage[:, n % 2, :]
                else:
                    src = W2[bass.ds(e, 1), (n - 2) * 512:(n - 1) * 512, :]\
                        .rearrange("e (c p) d -> p (e c) d", p=P)
                    dst = stage[:, n % 2, :].rearrange("p (c d) -> p c d", d=D)
                sp.dma_start(dst, src).then_inc(w_loaded[n % 2], 16)

            def rows(v):
                return v.rearrange("(a n) -> a n", a=1)

            load_x(0)
            load_ctx(0)
            for n, w in enumerate((Wq, Wk, Wv, Wo)):
                sp.dma_start(stage[:, n // 2, (n % 2) * 512:(n % 2 + 1) * 512].rearrange("p (a i) -> p a i", i=D),
                             w.rearrange("(a p) i -> p a i", p=P)).then_inc(s["wa_loaded"], 16)
            sp.dma_start(bias_rows[0:64, :], b1.rearrange("e (c p) -> (e c) p", p=P)).then_inc(s["bcols_loaded"], 16)
            sp.dma_start(delta, side).then_inc(s["small_in"], 16)
            sp.wait_ge(s["zeroed"], 1)
            sp.dma_start(rows32[0:E, :], b2).then_inc(s["small_in"], 16)
            for r, v in enumerate((bq, bk, bv)):
                sp.dma_start(rows32[E + r:E + r + 1, :], rows(v)).then_inc(s["small_in"], 16)
            sp.dma_start(rows32[E + 3:E + 4, 0:B], rows(tau)).then_inc(s["small_in"], 16)
            sp.dma_start(wr[:, :, :], Wr.rearrange("(k p) e -> p k e", p=P)).then_inc(s["small_in"], 16)
            for dst, src, n in ((tau4, tau, B), (brb, br, E), (bob, bo, D)):
                sp.dma_start(dst[:, :], rows(src).to_broadcast([P, n])).then_inc(s["small_in"], 16)
            sp.wait_ge(s["delta_split"], 1)
            for r in range(2):
                sp.dma_start(delta_dram[r], dparts[:, r, :]).then_inc(s["delta_stored"], 16)
            sp.wait_ge(s["rows_split"], 1)
            for r in range(2):
                sp.dma_start(rows_dram[r], rparts[:, r, :]).then_inc(s["rows_stored"], 16)
            sp.dma_start(xn2_dram[T:T + P, :], xn2[:, 0, :]).then_inc(s["zeros_stored"], 16)
            sp.dma_start(out[T:T + P, :], xn2[:, 0, :]).then_inc(s["zeros_stored"], 16)
            sp.wait_ge(s["rows_stored"], 32)
            sp.dma_start(qrow[0:2, :], rows_dram[0:1, E, :].to_broadcast([2, D])).then_inc(s["rows_in"], 16)
            sp.dma_start(qrow[2:3, :], rows_dram[1:2, E, :]).then_inc(s["rows_in"], 16)
            sp.dma_start(trow[0:2, :], rows_dram[:, E + 3, 0:B]).then_inc(s["rows_in"], 16)
            sp.dma_start(trow[2:3, :], rows_dram[0:1, E + 3, 0:B]).then_inc(s["rows_in"], 16)
            sp.dma_start(kvrow[:, :, :], rows_dram[:, E + 1:E + 3, :]).then_inc(s["rows_in"], 16)
            sp.wait_ge(s["delta_stored"], 32)
            sp.wait_ge(s["wT_ps"], 4)
            load_w(0, 0)
            load_w(0, 1)

            def put_x1(b, bb):
                sp.wait_ge(s["x1_ready"], b + 1)
                sp.dma_start(out[bass.ds(b * S, S), :], x1[:, bb, :]).then_inc(x1_stored[bb], 16)

            def put_xn2(b, bb):
                sp.wait_ge(s["xn2_ready"], b + 1)
                sp.dma_start(xn2_dram[bass.ds(b * S, S), :], xn2[:, bb, :]).then_inc(xn2_stored[bb], 16)

            def store_parts(dram, p, parts, name):
                for r, n in enumerate(parts):
                    sp.dma_start(dram[p, :, :, r].rearrange("j a i n -> (j a) i n"),
                                 qkc[:, n, :, :].rearrange("p k n -> p (k n)")).then_inc(s[name], 16)

            def load_stacks(dst, dram, p):
                for par in range(2):
                    sp.dma_start(dst[64 * par:64 * par + 3 * DK, p, :, :].rearrange("p (j c) n -> p j (c n)", c=2),
                                 dram[p, :, par].rearrange("j r i n -> (r i) j n")).then_inc(stack_ready[p], 16)

            def load_deltas(t, p):
                wait(sp, "st_ps", 8 * (t - 1))
                for par in range(2):
                    r = 64 * par + 3 * DK
                    src = delta_dram[:, bass.ds(t * 2, 2), :].rearrange("r b n -> r (b n)")
                    sp.dma_start(KS[r:r + 2, p, :, :],
                                 src.unsqueeze(1).to_broadcast([2, H // 2, 2 * S]))\
                      .then_inc(stack_ready[p], 16)

            def step(t, p):
                if has(t, 0, G):
                    load_deltas(t, p)
                if batch_in(t, 0, 2):
                    put_xn2(2 * t - 4, 0)
                if has(t, 0, E):
                    load_w(t, 2)
                    load_w(t, 3)
                if has(t, 0, G - 1):
                    load_ctx(t + 1)
                if batch_in(t, 0, 1):
                    put_x1(2 * t - 3, 1)
                if has(t, 0, G):
                    sp.wait_ge(s["ql_ready"], t + 1)
                    store_parts(q_dram, p, (0, 0, 1), "q_stored")
                    sp.wait_ge(s["kl_ready"], t + 1)
                    store_parts(k_dram, p, (2, 3, 2), "k_stored")
                    sp.wait_ge(s["ones_ready"], 1)
                    own_wait(sp, "q_stored", 48 * (t + 1))
                    load_stacks(QS, q_dram, p)
                    own_wait(sp, "k_stored", 48 * (t + 1))
                    load_stacks(KS, k_dram, p)
                if batch_in(t, 1, 2):
                    put_xn2(2 * t - 3, 1)
                if has(t, 0, G - 1):
                    load_x(t + 1)
                if has(t, 0, E - 1):
                    load_w(t + 1, 0)
                    load_w(t + 1, 1)
                if batch_in(t, 1, 1):
                    put_x1(2 * t - 2, 0)

            attention_steps(sp, step)
            sp.wait_ge(s["po_ps"], B)
            sp.dma_start(b2r, rows_dram[:, 0:E, :].rearrange("r e d -> r (e d)")).then_inc(s["b2_moved"], 16)

        @block.gpsimd
        def _(pool):
            link = chain(pool, "c_pool")
            for m in (ident, identh, trih):
                pool.memset(m[:, :], 0.0)
            pool.memset(sel[:, :], 0.0)
            pool.memset(onesh[:, :], 1.0)
            pool.memset(nhalf[:, :], -0.5)
            link(pool.memset(notfirst[:, :], 1.0))
            for m in (ident, identh):
                link(pool.affine_select(out=m[:, :], in_=m[:, :], compare_op=ALU.not_equal, fill=1.0,
                                        base=0, pattern=[[-1, P]], channel_multiplier=1))
            link(pool.affine_select(out=trih[:, :], in_=trih[:, :], compare_op=ALU.is_ge, fill=1.0,
                                    base=0, pattern=[[-1, P]], channel_multiplier=1))
            for base in (0, -H):
                link(pool.affine_select(out=sel[:, :], in_=sel[:, :], compare_op=ALU.not_equal,
                                        fill=1.0, base=base, pattern=[[-1, H]],
                                        channel_multiplier=1))
            link(pool.affine_select(out=notfirst[:, :], in_=notfirst[:, :], compare_op=ALU.not_equal,
                                    fill=0.0, base=0, pattern=[[0, E], [1, B]], channel_multiplier=0))

            def iota(dst, pattern, base, mult):
                return pool.iota(dst, pattern, base=base, channel_multiplier=mult,
                                 allow_small_or_imprecise_dtypes=True)

            iota(rev[:, :], [[-1, E]], E, 0)
            iota(steps[:, :], [[TW, B]], 0, 0)
            iota(tokval[:, :, :], [[0, 2], [S, B]], -T, 1)
            iota(slot_no[:, :], [[1, P]], 0, 0)
            iota(tile_no[:, :], [[1, NS]], 0, 0)
            iota(part_no[:, :], [[0, 1]], 0, 1).then_inc(s["const_ready"], 1)

            def piece_lo(e, n):
                h, l = ((w1h, w1l), (w2h, w2l))[n // 2]
                at = bass.ds(e * (KT * F) + (n % 2) * 1024, 1024)
                own_wait(pool, "w_hi", 4 * e + n + 1)
                pool.tensor_tensor(l[:, at], stage[:, n % 2, :], h[:, at], ALU.subtract).then_inc(s["w_lo"], 1)

            def x_plus_bo(g, p):
                pool.wait_ge(x_loaded, 16 * (g + 1))
                wait(pool, "x1_ready", 2 * g - 2)
                pool.tensor_tensor(xb[:, p, :, :], xin[:, :, :],
                                   bob[:, :].unsqueeze(1).to_broadcast([P, 2, D]), ALU.add)\
                    .then_inc(s["xb_ready"], 1)

            def exp_lo(b, u):
                pool.wait_ge(s["exp_done"], 4 * b + u + 1)
                pool.tensor_tensor(PL[:, 4 * u:4 * u + 4, :].rearrange("p h n -> p (h n)"), P32[:, 0, :],
                                   PH[:, 4 * u:4 * u + 4, :].rearrange("p h n -> p (h n)"), ALU.subtract)\
                    .then_inc(s["pl_even"], 1)

            def rstd_1(g):
                link = chain(pool, "c_rs1", g)
                own_wait(pool, "ln1_stats", g + 1)
                link(pool.tensor_scalar(rs1[:, 0, :], mv1[:, :, 1], EPS, None, ALU.add))
                pool.tensor_tensor(rs1[:, 1, :], rs1[:, 0, :], nhalf[:, :], ALU.pow).then_inc(s["rstd1"], 1)

            def rstd_2(b):
                link = chain(pool, "c_rs2", b)
                own_wait(pool, "ln2_stats", b + 1)
                link(pool.tensor_scalar(rs2[:, 0:1], mv2[:, 1:2], EPS, None, ALU.add))
                pool.tensor_tensor(rs2[:, 1:2], rs2[:, 0:1], nhalf[:, 0:1], ALU.pow).then_inc(s["rstd2"], 1)

            rstd_1(0)

            pool.wait_ge(s["small_in"], 16 * SMALL)

            def step(t, p):
                for bb in range(2):
                    b = 2 * t - 2 + bb
                    if has(t, 0, E):
                        piece_lo(t, 2 * bb)
                        piece_lo(t, 2 * bb + 1)
                    if bb == 1 and has(t, 0, G):
                        x_plus_bo(t, p)
                    if batch_in(t, bb, 0):
                        exp_lo(b, 0)
                    if batch_in(t, bb, 1):
                        rstd_2(b - 1)
                    if batch_in(t, bb, 0):
                        exp_lo(b, 2)
                    if bb == 1 and has(t, 0, G - 1):
                        rstd_1(t + 1)

            attention_steps(pool, step)

            pool.wait_ge(s["routed"], 1)
            pool.wait_ge(s["zeros_stored"], 32)
            for i in range(2):
                pool.wait_ge(x1_stored[i], 16 * G)
                pool.wait_ge(xn2_stored[i], 16 * G)

            def gather(j, p):
                wait(pool, "gT_ps", j - 1)
                pool.tensor_copy(idxg[:, 2 * p:2 * p + 2], slot_rows[:, bass.ds(j * 2, 2)]).then_inc(s["idxg_ready"], 1)
                own_wait(pool, "idxg_ready", j + 1)
                for i in range(2):
                    pool.indirect_dma_start(out=xs[p][:, i, :], out_offset=None, in_=xn2_dram,
                                            in_offset=bass.IndirectOffsetOnAxis(ap=idxg[:, 2 * p + i:2 * p + i + 1], axis=0))\
                        .then_inc(rows_in[p], 16)

            def scatter(j, p):
                pool.wait_ge(s["yy_ready"], j + 1)
                wait(pool, "added", 32 * j)
                pool.tensor_copy(idxs, slot_rows[:, bass.ds(j * 2, 2)]).then_inc(s["idxs_ready"], 1)
                own_wait(pool, "idxs_ready", j + 1)
                for i in range(2):
                    if i:
                        own_wait(pool, "added", 32 * j + 16)
                    pool.indirect_dma_start(out=out, out_offset=bass.IndirectOffsetOnAxis(ap=idxs[:, i:i + 1], axis=0),
                                            in_=yw[p][:, i, :], in_offset=None, compute_op=ALU.add)\
                        .then_inc(s["added"], 16)

            gather(0, 0)
            gather(1, 1)

            def step(t, p):
                if has(t, 0, NT - 2):
                    gather(t + 2, p)
                if has(t, 2, NT + 2):
                    scatter(t - 2, p)

            expert_steps(pool, step)
            pool.wait_ge(s["added"], 32 * NT)

        @block.scalar
        def _(act):
            def copy(dst, src):
                return act.activation(dst, src, ACT.Copy)

            for n in range(4):
                act.wait_ge(s["wT_ps"], n + 1)
                copy(wah[:, n, :, :], banks[n][:, :].rearrange("p (k n) -> p k n", k=KT)).then_inc(s["wT_hi"], 1)
            act.wait_ge(s["bc_ps"], 1)
            copy(bcols[:, :], pA[:, 0:E * FC]).then_inc(s["bc_ready"], 1)

            def piece_hi(e, n):
                at = bass.ds(e * (KT * F) + (n % 2) * 1024, 1024)
                act.wait_ge(w_loaded[n % 2], 32 * e + 16 * (n // 2 + 1))
                copy((w1h, w2h)[n // 2][:, at], stage[:, n % 2, :]).then_inc(s["w_hi"], 1)

            def x_hi(g):
                act.wait_ge(s["xT_ps"], g + 1)
                copy(xT[:, 0, :, :], pA[:, :].rearrange("p (k n) -> p k n", k=KT)).then_inc(s["xh_ready"], 1)

            def ctx_hi(g):
                act.wait_ge(s["cT_ps"], g + 1)
                copy(xT[:, 2, :, :], pB[:, :].rearrange("p (k n) -> p k n", k=KT)).then_inc(s["ch_ready"], 1)

            def qk_hi(g, n, ps, name):
                act.wait_ge(s[name + "_ps"], g + 1)
                wait(act, name + "_stored", 48 * g)
                copy(qkc[:, n, :, :], ps[:, :].rearrange("p (k n) -> p k n", k=KT)).then_inc(s[name + "h_ready"], 1)

            def v_hi(g, p):
                act.wait_ge(s["v_ps"], g + 1)
                wait(act, "po_ps", 2 * (g - 1))
                copy(V[:, 0, p, :, :, 0:DK], pA[:, :].rearrange("p (b h d) -> p b h d", b=2, d=DK))\
                    .then_inc(s["vh_ready"], 1)

            def exps(b, u):
                if u == 0:
                    wait(act, "po_ps", b)
                wait(act, ("pl_even", "pl_odd")[u % 2], 2 * b + u // 2)
                act.wait_ge(s["st_ps"], 4 * b + u + 1)
                act.activation(P32[:, u % 2, :], psST[u % 2][:, :], ACT.Exp)
                act.activation(PH[:, 4 * u:4 * u + 4, :], psST[u % 2][:, :].rearrange("p (h n) -> p h n", h=4), ACT.Exp)\
                    .then_inc(s["exp_done"], 1)

            def oT_hi(b):
                act.wait_ge(s["oT_ps"], b + 1)
                copy(oT[:, 0, :, :], pT6).then_inc(s["oh_ready"], 1)

            def xn2_T(b):
                act.wait_ge(s["x2T_ps"], b + 1)
                copy(xn2T[:, :, :], pT6).then_inc(s["x2T_ready"], 1)

            def step(t, p):
                for bb in range(2):
                    b = 2 * t - 2 + bb
                    new, att = has(t, 0, G), batch_in(t, bb, 0)
                    if new:
                        piece_hi(t, 2 * bb)
                        piece_hi(t, 2 * bb + 1)
                    if bb == 0 and new:
                        x_hi(t)
                        ctx_hi(t)
                    if bb == 1 and new:
                        v_hi(t, p)
                    if batch_in(t, bb, 1):
                        oT_hi(b - 1)
                    if att:
                        act.wait_ge(s["mT_ps"], b + 1)
                        copy(mT[:, :], pM[0:2 * H, :]).then_inc(s["mT_ready"], 1)
                        exps(b, 0)
                        exps(b, 1)
                    if bb == 0 and new:
                        qk_hi(t, 0, pA, "q")
                    if att:
                        exps(b, 2)
                    if bb == 0 and new:
                        qk_hi(t, 2, pB, "k")
                    if batch_in(t, bb, 2):
                        xn2_T(b - 2)
                    if att:
                        exps(b, 3)

            attention_steps(act, step)

            act.wait_ge(s["gap_ready"], 1)
            act.activation(rb[:, 5, :], rb[:, 4, :], ACT.Exp).then_inc(s["e_ready"], 1)
            act.wait_ge(s["routed"], 1)

            def step(t, p):
                if has(t, 0, NT):
                    act.wait_ge(s["gT_ps"], t + 1)
                    copy(xT[:, 2 * p, :, :], (pA, pB)[p][:, :].rearrange("p (k n) -> p k n", k=KT))\
                        .then_inc(s["gh_ready"], 1)
                if has(t, 1, NT + 1):
                    j = t - 1
                    e = act.value_load(tile_exp[0:1, bass.ds(j, 1)], min_val=0, max_val=E - 1)
                    for u in range(4):
                        wait(act, "hl_done", 4 * j + u - 3)
                        act.wait_ge(s["h_ps"], 4 * j + u + 1)
                        for c in range(2):
                            ins = act.activation(hid[u][:, c * TW:(c + 1) * TW], banks[u][:, c * TW:(c + 1) * TW],
                                                 ACT.Gelu_apprx_tanh, bias=bcols[:, bass.ds(e * FC + 2 * u + c, 1)])
                        ins.then_inc(s["gelu_done"], 1)

            expert_steps(act, step)

        @block.vector
        def _(dve):
            link = chain(dve, "c_setup")
            dve.memset(rows32, 0.0)
            dve.memset(xn2[:, 0, :], 0.0).then_inc(s["zeroed"], 1)
            dve.memset(V[:, 0, :, :, :, DK], 1.0)
            dve.memset(V[:, 1, :, :, :, DK], 0.0)
            dve.memset(QS[:, :, :, :], 1.0).then_inc(s["ones_ready"], 1)
            dve.wait_ge(s["small_in"], 16 * SMALL)
            link(dve.tensor_scalar(tau4[:, :], tau4[:, :], DK ** -0.5, None, ALU.mult))
            link(dve.tensor_scalar(delta, delta, DK ** -0.5, None, ALU.mult))
            link(dve.tensor_copy(dparts[:, 0, :], delta))
            dve.tensor_tensor(dparts[:, 1, :], delta, dparts[:, 0, :], ALU.subtract)\
                .then_inc(s["delta_split"], 1)
            link(dve.tensor_copy(rparts[:, 0, :], rows32))
            dve.tensor_tensor(rparts[:, 1, :], rows32, rparts[:, 0, :], ALU.subtract)\
                .then_inc(s["rows_split"], 1)
            dve.wait_ge(s["zeros_stored"], 32)

            def ln_1_stats(g):
                dve.wait_ge(x_loaded, 16 * (g + 1))
                for i in range(2):
                    ins = dve.bn_stats(st1[:, i, :], xin[:, i, :])
                ins.then_inc(s["c_ln1"], 1)
                own_wait(dve, "c_ln1", 2 * g + 1)
                for i in range(2):
                    ins = dve.bn_aggr(mv1[:, i, :], st1[:, i, :])
                ins.then_inc(s["ln1_stats"], 1)

            def ln_1(g):
                dve.wait_ge(s["rstd1"], g + 1)
                dve.tensor_tensor(rs1[:, 2, :], rs1[:, 1, :], tau4[:, bass.ds(g * 2, 2)], ALU.mult)\
                    .then_inc(s["c_ln1"], 1)
                dve.wait_ge(s["c_ln1"], 2 * g + 2)
                wait(dve, "xT_ps", g)
                for i in range(2):
                    ins = dve.tensor_scalar(xn[:, i, :], xin[:, i, :], mv1[:, i, 0:1], rs1[:, 2, i:i + 1],
                                            ALU.subtract, ALU.mult)
                ins.then_inc(s["xn_ready"], 1)

            def k2(v):
                return v.rearrange("p (k n) -> p k n", k=KT)

            ln_1_stats(0)
            ln_1(0)
            for n in range(4):
                dve.wait_ge(s["wT_hi"], n + 1)
                dve.tensor_tensor(wal[:, n, :, :], k2(banks[n][:, :]), wah[:, n, :, :], ALU.subtract)\
                    .then_inc(s["wT_lo"], 1)
            dve.wait_ge(s["rows_in"], 16 * 5)
            dve.tensor_scalar(trow[:, :], trow[:, :], DK ** -0.5, None, ALU.mult).then_inc(s["tau_ready"], 1)

            def x_lo(g):
                dve.wait_ge(s["xh_ready"], g + 1)
                dve.tensor_tensor(xT[:, 1, :, :], k2(pA[:, :]), xT[:, 0, :, :], ALU.subtract)\
                    .then_inc(s["xl_ready"], 1)

            def ctx_lo(g):
                dve.wait_ge(s["ch_ready"], g + 1)
                dve.tensor_tensor(xT[:, 3, :, :], k2(pB[:, :]), xT[:, 2, :, :], ALU.subtract)\
                    .then_inc(s["cl_ready"], 1)

            def qk_lo(g, n, ps, name):
                dve.wait_ge(s[name + "h_ready"], g + 1)
                dve.tensor_tensor(qkc[:, n + 1, :, :], k2(ps[:, :]), qkc[:, n, :, :], ALU.subtract)\
                    .then_inc(s[name + "l_ready"], 1)

            def v_lo(g, p):
                dve.wait_ge(s["vh_ready"], g + 1)
                dve.tensor_tensor(V[:, 1, p, :, :, 0:DK], pA[:, :].rearrange("p (b h d) -> p b h d", b=2, d=DK),
                                  V[:, 0, p, :, :, 0:DK], ALU.subtract).then_inc(s["vl_ready"], 1)

            def maxima(b, u):
                dve.wait_ge(s["s_ps"], 4 * b + u + 1)
                dve.reduce_max(mx[:, 4 * u:4 * u + 4], psS[u % 2][:, :].rearrange("p (h n) -> p h n", h=4),
                               AX.X).then_inc(s["m_red"], 1)

            def maxima_out(b):
                dve.wait_ge(s["m_red"], 4 * b + 4)
                wait(dve, "mT_ps", b)
                dve.tensor_scalar(mm[:, 0:H], mx[:, :], -1.0, None, ALU.mult).then_inc(s["c_mm"], 1)
                dve.wait_ge(s["c_mm"], b + 1)
                dve.scalar_tensor_tensor(out=mm[:, H:2 * H], in0=mx[:, :], scalar=-1.0, in1=mm[:, 0:H],
                                         op0=ALU.mult, op1=ALU.subtract).then_inc(s["mm_ready"], 1)

            def exp_lo(b, u):
                dve.wait_ge(s["exp_done"], 4 * b + u + 1)
                dve.tensor_tensor(PL[:, 4 * u:4 * u + 4, :].rearrange("p h n -> p (h n)"), P32[:, 1, :],
                                  PH[:, 4 * u:4 * u + 4, :].rearrange("p h n -> p (h n)"), ALU.subtract)\
                    .then_inc(s["pl_odd"], 1)

            def heads_out(b):
                dve.wait_ge(s["po_ps"], b + 1)
                dve.reciprocal(rec[:, :], pO[:, :, DK]).then_inc(s["c_on"], 1)
                dve.wait_ge(s["c_on"], b + 1)
                wait(dve, "oT_ps", b)
                dve.tensor_tensor(on[:, :, :], pO[:, :, 0:DK], rec[:, :].unsqueeze(2).to_broadcast([P, H, DK]),
                                  ALU.mult).then_inc(s["on_ready"], 1)

            def oT_lo(b):
                dve.wait_ge(s["oh_ready"], b + 1)
                dve.tensor_tensor(oT[:, 1, :, :], pT6, oT[:, 0, :, :], ALU.subtract).then_inc(s["ol_ready"], 1)

            def residual(b, bb, p):
                dve.wait_ge(s["y_ps"], b + 1)
                wait(dve, x1_stored[bb], 8 * (b - bb))
                dve.tensor_tensor(x1[:, bb, :], pY6, xb[:, p, bb, :], ALU.add).then_inc(s["x1_ready"], 1)
                dve.wait_ge(s["x1_ready"], b + 1)
                dve.bn_stats(st2[:, :], x1[:, bb, :]).then_inc(s["c_ln2"], 1)
                own_wait(dve, "c_ln2", b + 1)
                dve.bn_aggr(mv2[:, :], st2[:, :]).then_inc(s["ln2_stats"], 1)

            def ln_2(b, bb):
                dve.wait_ge(s["rstd2"], b + 1)
                wait(dve, xn2_stored[bb], 8 * (b - bb))
                dve.tensor_scalar(xn2[:, bb, :], x1[:, bb, :], mv2[:, 0:1], rs2[:, 1:2],
                                  ALU.subtract, ALU.mult).then_inc(s["xn2_ready"], 1)

            def score(b):
                dve.wait_ge(s["r_ps"], b + 1)
                dve.tensor_tensor(sc[:, :, bass.ds(b, 1)], pR.unsqueeze(2), brb[:, :].unsqueeze(2), ALU.add)\
                    .then_inc(s["sc_ready"], 1)

            def step(t, p):
                for bb in range(2):
                    b = 2 * t - 2 + bb
                    new, att = has(t, 0, G), batch_in(t, bb, 0)
                    if att:
                        maxima(b, 0)
                        maxima(b, 1)
                    if batch_in(t, bb, 2):
                        ln_2(b - 2, bb)
                    if batch_in(t, bb, 1):
                        heads_out(b - 1)
                    if att:
                        maxima(b, 2)
                        maxima(b, 3)
                        maxima_out(b)
                    if bb == 0 and new:
                        x_lo(t)
                        ctx_lo(t)
                    if bb == 1 and new:
                        v_lo(t, p)
                    if batch_in(t, bb, 1):
                        oT_lo(b - 1)
                    if att:
                        exp_lo(b, 1)
                    if batch_in(t, bb, 1):
                        residual(b - 1, 1 - bb, p if bb == 0 else 1 - p)
                    if bb == 0 and new:
                        qk_lo(t, 0, pA, "q")
                        qk_lo(t, 2, pB, "k")
                    if bb == 1 and has(t, 0, G - 1):
                        ln_1_stats(t + 1)
                    if att:
                        exp_lo(b, 3)
                    if batch_in(t, bb, 2):
                        score(b - 2)
                    if bb == 1 and has(t, 0, G - 1):
                        ln_1(t + 1)

            attention_steps(dve, step)
            dve.wait_ge(s["sc_ready"], B)
            dve.wait_ge(s["const_ready"], 1)

            link = chain(dve, "c_route")

            def over_experts(v):
                return v.rearrange("p e b -> p b e")

            def per_batch(v):
                return v.unsqueeze(1).to_broadcast([P, E, B])

            scores = sc[:, :, :]
            for k in range(2):
                best, first = rb[:, k, :], rb[:, 2 + k, :]
                link(dve.reduce_max(best, over_experts(scores), AX.X))
                link(dve.tensor_tensor(ra[:, 0, :, :], scores, per_batch(best), ALU.is_equal))
                link(dve.tensor_tensor(ra[:, 0, :, :], ra[:, 0, :, :], rev[:, :].unsqueeze(2).to_broadcast([P, E, B]),
                                       ALU.mult))
                link(dve.reduce_max(first, over_experts(ra[:, 0, :, :]), AX.X))
                link(dve.tensor_tensor(hot[:, k, :, :], ra[:, 0, :, :], per_batch(first), ALU.is_equal))
                if k == 0:
                    link(dve.scalar_tensor_tensor(out=ra[:, 1, :, :], in0=hot[:, 0, :, :], scalar=-3.0e38,
                                                  in1=scores, op0=ALU.mult, op1=ALU.add))
                    scores = ra[:, 1, :, :]
            dve.tensor_tensor(rb[:, 4, :], rb[:, 1, :], rb[:, 0, :], ALU.subtract).then_inc(s["gap_ready"], 1)
            mask3 = mask[:, :].rearrange("p (e b) -> p e b", e=E)
            dve.tensor_tensor(mask3, hot[:, 0, :, :], hot[:, 1, :, :], ALU.add).then_inc(s["mask_ready"], 1)
            dve.wait_ge(s["e_ready"], 1)
            link(dve.tensor_scalar(rb[:, 6, :], rb[:, 5, :], 1.0, None, ALU.add))
            pw = rb[:, 6:8, :]
            link(dve.reciprocal(rb[:, 6, :], rb[:, 6, :]))
            link(dve.tensor_tensor(rb[:, 7, :], rb[:, 5, :], rb[:, 6, :], ALU.mult))
            link(dve.tensor_copy(vals[:, 1, :].rearrange("p (c b) -> p c b", c=2), pw))
            dve.tensor_copy(vals[:, 0, :].rearrange("p (c b) -> p c b", c=2), tokval[:, :, :])
            link(dve.tensor_tensor(vals[:, 2, :].rearrange("p (c b) -> p c b", c=2), pw,
                                   vals[:, 1, :].rearrange("p (c b) -> p c b", c=2), ALU.subtract))
            ranks, counts = pA[:, 0:P], pA[:, P:2 * P]
            flat = [ra[:, i, :, :].rearrange("p e b -> p (e b)") for i in range(3)]
            dve.wait_ge(s["rank_ps"], 1)
            link(dve.tensor_tensor_scan(flat[0], notfirst[:, :], counts, 0.0, ALU.mult, ALU.add))
            link(dve.tensor_tensor(ra[:, 1, :, :], ra[:, 0, :, B - 1:B].to_broadcast([P, E, B]),
                                   steps[:, :].unsqueeze(1).to_broadcast([P, E, B]), ALU.is_gt))
            link(dve.reduce_sum(rc[:, 0, :], ra[:, 1, :, :], AX.X))
            link(dve.tensor_tensor_scan(rc[:, 1, :], onesh[:, 0:E], rc[:, 0, :], 0.0, ALU.mult, ALU.add))
            link(dve.tensor_tensor(rc[:, 2, :], rc[:, 1, :], rc[:, 0, :], ALU.subtract))
            link(dve.tensor_tensor(flat[0], flat[0], counts, ALU.subtract))
            link(dve.tensor_tensor(flat[0], flat[0], ranks, ALU.add))
            link(dve.scalar_tensor_tensor(out=ra[:, 2, :, :], in0=rc[:, 2, :].unsqueeze(2).to_broadcast([P, E, B]),
                                          scalar=float(TW), in1=ra[:, 0, :, :], op0=ALU.mult, op1=ALU.add))
            for k in range(2):
                link(dve.tensor_tensor(ra[:, k, :, :], hot[:, k, :, :], ra[:, 2, :, :], ALU.mult))
                link(dve.reduce_sum(pos[:, k, :], over_experts(ra[:, k, :, :]), AX.X))
            link(dve.tensor_copy(posi[:, 0, :], pos[:, :, :].rearrange("p c b -> p (c b)")))
            link(dve.tensor_scalar(posi[:, 1, :], posi[:, 0, :], 7, None, ALU.arith_shift_right))
            link(dve.tensor_scalar(posi[:, 2, :], posi[:, 0, :], P - 1, None, ALU.bitwise_and))
            link(dve.tensor_copy(posf[:, :, :], posi[:, 1:3, :]))
            link(dve.tensor_tensor(hot_tile, tile_no[:, :].unsqueeze(1).to_broadcast([P, 2 * B, NS]),
                                   posf[:, 0, :].unsqueeze(2).to_broadcast([P, 2 * B, NS]), ALU.is_equal))
            for v in range(3):
                dve.tensor_tensor(hot_val[:, :, v, :], hot_tile,
                                  vals[:, v, :].unsqueeze(2).to_broadcast([P, 2 * B, NS]), ALU.mult)
            dve.tensor_tensor(hot_slot, slot_no[:, :].unsqueeze(1).to_broadcast([P, 2 * B, P]),
                              posf[:, 1, :].unsqueeze(2).to_broadcast([P, 2 * B, P]), ALU.is_equal)\
                .then_inc(s["hot_ready"], 1)
            link(dve.tensor_tensor(tile_e, rc[0:1, 1, :].unsqueeze(1).to_broadcast([1, NT, E]),
                                   tile_no[0:1, 0:NT].unsqueeze(2).to_broadcast([1, NT, E]), ALU.is_le))
            link(dve.reduce_sum(tile_f, tile_e, AX.X))
            link(dve.tensor_scalar(tile_exp, tile_f, float(E - 1), None, ALU.min))
            dve.wait_ge(s["slot_ps"], 1)
            link(dve.tensor_copy(slot_t[:, :, :], pB[:, 0:2 * NS].rearrange("p (a j) -> p a j", a=2)))
            link(dve.tensor_tensor(slot_w, slot_t[:, 1, :], pB[:, 2 * NS:3 * NS], ALU.add))
            link(dve.tensor_scalar(slot_t[:, 1, :], slot_t[:, 0, :], 0.0, part_no[:, 0:1], ALU.is_equal, ALU.mult))
            dve.scalar_tensor_tensor(out=slot_rows[:, :], in0=slot_t[:, 0, :], scalar=float(T),
                                     in1=slot_t[:, 1, :], op0=ALU.add, op1=ALU.add).then_inc(s["routed"], 1)

            def step(t, p):
                if has(t, 0, NT):
                    dve.wait_ge(s["gh_ready"], t + 1)
                    dve.tensor_tensor(xT[:, 2 * p + 1, :, :], k2((pA, pB)[p][:, :]), xT[:, 2 * p, :, :],
                                      ALU.subtract).then_inc(s["gl_ready"], 1)
                if has(t, 1, NT + 1):
                    j, q = t - 1, 1 - p
                    wait(dve, "yy_ps", j - 1)
                    for u in range(4):
                        dve.wait_ge(s["gelu_done"], 4 * j + u + 1)
                        parts = [v[q][:, 2 * u:2 * u + 2, :].rearrange("p c n -> p (c n)") for v in (hh, hl)]
                        dve.tensor_copy(parts[0], hid[u]).then_inc(s["hh_done"], 1)
                        own_wait(dve, "hh_done", 4 * j + u + 1)
                        dve.tensor_tensor(parts[1], hid[u], parts[0], ALU.subtract).then_inc(s["hl_done"], 1)
                if has(t, 2, NT + 2):
                    j = t - 2
                    dve.wait_ge(s["yy_ps"], j + 1)
                    wait(dve, "added", 32 * (j - 1))
                    for i in range(2):
                        ins = dve.tensor_scalar(yw[p][:, i, :], banks[6 + p][:, i * D:(i + 1) * D],
                                                slot_w[:, bass.ds(j * 2 + i, 1)], None, ALU.mult)
                    ins.then_inc(s["yy_ready"], 1)

            expert_steps(dve, step)

        @block.tensor
        def _(pe):
            def split_product(ps, lhs, rhs, first=True, last=True):
                for k in range(KT):
                    for i, (a, b_) in enumerate(((0, 0), (0, 1), (1, 0))):
                        ins = pe.matmul(ps, lhs(a, k), rhs(b_, k), start=first and k == 0 and i == 0,
                                        stop=last and k == KT - 1 and i == 2)
                return ins

            wa = (wah, wal)
            pe.wait_ge(s["const_ready"], 1)
            pe.wait_ge(s["wa_loaded"], 64)
            for n in range(4):
                for k in range(KT):
                    for a in range(2):
                        ins = pe.transpose(banks[n][:, k * D + a * P:k * D + (a + 1) * P],
                                           stage[:, n // 2, (n % 2) * 512 + a * D + k * P:(n % 2) * 512 + a * D + (k + 1) * P], ident[:, :])
                ins.then_inc(s["wT_ps"], 1)
            pe.wait_ge(s["bcols_loaded"], 16)
            pe.transpose(pA[:, 0:E * FC], bias_rows[0:E * FC, :], ident[0:E * FC, 0:E * FC]).then_inc(s["bc_ps"], 1)

            def turn(g, p):
                pe.wait_ge(s["xn_ready"], g + 1)
                wait(pe, "vl_ready", g)
                if known(g) and g == 0:
                    pe.wait_ge(s["bc_ready"], 1)
                for k in range(KT):
                    for i in range(2):
                        ins = pe.transpose(pA[:, (2 * k + i) * P:(2 * k + i + 1) * P],
                                           xn[:, i, k * P:(k + 1) * P], ident[:, :])
                ins.then_inc(s["xT_ps"], 1)
                pe.wait_ge(c_loaded, 16 * (g + 1))
                wait(pe, "kl_ready", g)
                for k in range(KT):
                    for i in range(2):
                        ins = pe.transpose(pB[:, (2 * k + i) * P:(2 * k + i + 1) * P],
                                           cin[:, i, k * P:(k + 1) * P], ident[:, :])
                ins.then_inc(s["cT_ps"], 1)

            def project_q(g):
                pe.wait_ge(s["xl_ready"], g + 1)
                if known(g) and g == 0:
                    pe.wait_ge(s["tau_ready"], 1)
                for c in range(KT):
                    o = pA[:, c * 2 * S:(c + 1) * 2 * S]
                    pe.matmul(o, qrow[:, c * P:(c + 1) * P],
                              trow[:, bass.ds(g * 2, 2)].unsqueeze(2).to_broadcast([3, 2, S]),
                              start=True, stop=False)
                    ins = split_product(o, lambda a, k: wa[a][:, 0, k, c * P:(c + 1) * P],
                                        lambda a, k: xT[:, a, k, :], first=False)
                ins.then_inc(s["q_ps"], 1)

            def project_k(g):
                pe.wait_ge(s["cl_ready"], g + 1)
                for c in range(KT):
                    o = pB[:, c * 2 * S:(c + 1) * 2 * S]
                    pe.matmul(o, kvrow[:, 0, c * P:(c + 1) * P], onesh[0:2, 0:1].to_broadcast([2, 2 * S]),
                              start=True, stop=False)
                    ins = split_product(o, lambda a, k: wa[a][:, 1, k, c * P:(c + 1) * P],
                                        lambda a, k: xT[:, 2 + a, k, :], first=False)
                ins.then_inc(s["k_ps"], 1)

            def project_v(g):
                pe.wait_ge(s["ql_ready"], g + 1)
                for i in range(2):
                    o = pA[:, i * D:(i + 1) * D]
                    pe.matmul(o, onesh[0:2, :], kvrow[:, 1, :], start=True, stop=False)
                    ins = split_product(o, lambda a, k: xT[:, 2 + a, k, i * S:(i + 1) * S],
                                        lambda a, k: wa[a][:, 2, k, :], first=False)
                ins.then_inc(s["v_ps"], 1)

            def scores(b, bb, p, u, keys_first):
                r = 64 * (u % 2)
                ps = (psST if keys_first else psS)[u % 2]
                wait(pe, "exp_done" if keys_first else "m_red", 4 * b + u - 1)
                for i in range(4):
                    j = 4 * (u // 2) + i
                    q = QS[r:r + ROWS, p, j, bb * S:(bb + 1) * S]
                    k = KS[r:r + ROWS, p, j, bb * S:(bb + 1) * S]
                    o = ps[:, i * S:(i + 1) * S]
                    if keys_first:
                        pe.matmul(o, k, q, start=True, stop=False)
                        ins = pe.matmul(o, sel[:, 4 * u + i:4 * u + i + 1].to_broadcast([2 * H, S]), mT[:, :],
                                        start=False, stop=True)
                    else:
                        ins = pe.matmul(o, q, k, start=True, stop=True)
                ins.then_inc(s["st_ps" if keys_first else "s_ps"], 1)

            def values(b, bb, p):
                pe.wait_ge(s["pl_even"], 2 * b + 2)
                pe.wait_ge(s["pl_odd"], 2 * b + 2)
                for k in range(H):
                    h = head_of(k)
                    for w, r in ((PH, 0), (PH, 1), (PL, 0)):
                        ins = pe.matmul(pO[:, h, :], w[:, k, :], V[:, r, p, bb, h, :],
                                        start=(w is PH and r == 0), stop=(w is PL))
                ins.then_inc(s["po_ps"], 1)

            def turn_heads(b):
                pe.wait_ge(s["on_ready"], b + 1)
                wait(pe, "sc_ready", b - 1)
                for k in range(KT):
                    ins = pe.transpose(pT6[:, k, :], on[:, :, :].rearrange("p h d -> p (h d)")[:, k * P:(k + 1) * P],
                                       ident[:, :])
                ins.then_inc(s["oT_ps"], 1)

            def out_product(b):
                pe.wait_ge(s["ol_ready"], b + 1)
                split_product(pY6, lambda a, k: oT[:, a, k, :], lambda a, k: wa[a][:, 3, k, :])\
                    .then_inc(s["y_ps"], 1)

            def turn_xn2(b, bb):
                pe.wait_ge(s["xn2_ready"], b + 1)
                wait(pe, "x1_ready", b + 2 if not known(b) else min(b + 2, B))
                for k in range(KT):
                    ins = pe.transpose(pT6[:, k, :], xn2[:, bb, k * P:(k + 1) * P], ident[:, :])
                ins.then_inc(s["x2T_ps"], 1)

            def route(b):
                pe.wait_ge(s["x2T_ready"], b + 1)
                for k in range(KT):
                    ins = pe.matmul(pR, xn2T[:, k, :], wr[:, k, :], start=(k == 0), stop=(k == KT - 1))
                ins.then_inc(s["r_ps"], 1)

            pe.wait_ge(s["small_in"], 16 * SMALL)
            pe.wait_ge(s["wT_lo"], 4)

            def step(t, p):
                for bb in range(2):
                    b = 2 * t - 2 + bb
                    new, att = has(t, 0, G), batch_in(t, bb, 0)
                    q = 1 - p
                    if att:
                        if bb == 0:
                            pe.wait_ge(stack_ready[q], 6 * 8 * (t - 1 - q) + 6 * 16)
                        scores(b, bb, q, 0, False)
                        scores(b, bb, q, 1, False)
                    if batch_in(t, bb, 1):
                        if bb == 1:
                            pe.wait_ge(s["vl_ready"], t)
                        values(b - 1, 1 - bb, p if bb == 0 else q)
                    if att:
                        scores(b, bb, q, 2, False)
                        scores(b, bb, q, 3, False)
                    if bb == 0 and new:
                        turn(t, p)
                    if bb == 1 and new:
                        project_v(t)
                    if batch_in(t, bb, 1):
                        turn_heads(b - 1)
                    if att:
                        pe.wait_ge(s["mm_ready"], b + 1)
                        pe.transpose(pM[0:2 * H, :], mm[:, :], identh[:, :]).then_inc(s["mT_ps"], 1)
                        pe.wait_ge(s["mT_ready"], b + 1)
                        scores(b, bb, q, 0, True)
                        scores(b, bb, q, 1, True)
                    if batch_in(t, bb, 1):
                        out_product(b - 1)
                    if bb == 0 and new:
                        project_q(t)
                    if att:
                        scores(b, bb, q, 2, True)
                    if bb == 0 and new:
                        project_k(t)
                    if batch_in(t, bb, 2):
                        turn_xn2(b - 2, bb)
                    if att:
                        scores(b, bb, q, 3, True)
                    if batch_in(t, bb, 2):
                        route(b - 2)

            attention_steps(pe, step)

            pe.wait_ge(s["mask_ready"], 1)
            pe.matmul(pA[:, 0:P], trih[:, :], mask[:, :], start=True, stop=True)
            pe.matmul(pA[:, P:2 * P], onesh[:, :], mask[:, :], start=True, stop=True).then_inc(s["rank_ps"], 1)
            pe.wait_ge(s["hot_ready"], 1)
            for i in range(2 * B):
                ins = pe.matmul(pB[:, 0:3 * NS], hot_slot[:, i, :],
                                hot_val[:, i, :, :].rearrange("p v j -> p (v j)"),
                                start=(i == 0), stop=(i == 2 * B - 1))
            ins.then_inc(s["slot_ps"], 1)
            pe.wait_ge(s["w_lo"], 4 * E)
            pe.wait_ge(s["b2_moved"], 16)
            pe.wait_ge(s["routed"], 1)

            def step(t, p):
                q = 1 - p
                if has(t, 1, NT + 1):
                    e1 = pe.value_load(tile_exp[0:1, bass.ds(t - 1, 1)], min_val=0, max_val=E - 1)
                if has(t, 2, NT + 2):
                    e2 = pe.value_load(tile_exp[0:1, bass.ds(t - 2, 1)], min_val=0, max_val=E - 1)
                if has(t, 0, NT):
                    pe.wait_ge(rows_in[p], 16 * (t - p) + 32)
                    wait(pe, "gl_ready", t - 1)
                    for k in range(KT):
                        for i in range(2):
                            ins = pe.transpose((pA, pB)[p][:, (2 * k + i) * P:(2 * k + i + 1) * P],
                                               xs[p][:, i, k * P:(k + 1) * P], ident[:, :])
                    ins.then_inc(s["gT_ps"], 1)
                if has(t, 1, NT + 1):
                    j = t - 1
                    pe.wait_ge(s["gl_ready"], j + 1)
                    for u in range(4):
                        wait(pe, "gelu_done", 4 * j + u - 3)
                        for c in range(2):
                            at = (2 * u + c) * P
                            ins = split_product(banks[u][:, c * TW:(c + 1) * TW],
                                                lambda a, k: (w1h, w1l)[a][:, bass.ds(e1 * (KT * F) + k * F + at, P)],
                                                lambda a, k: xT[:, 2 * q + a, k, :])
                        ins.then_inc(s["h_ps"], 1)
                if has(t, 2, NT + 2):
                    j = t - 2
                    pe.wait_ge(s["hl_done"], 4 * j + 4)
                    wait(pe, "yy_ready", j - 1)
                    for i in range(2):
                        ps = banks[6 + p][:, i * D:(i + 1) * D]
                        pe.matmul(ps, onesh[0:2, :], b2r[:, bass.ds(e2 * D, D)], start=True, stop=False)
                        for c in range(FC):
                            for a, b_ in ((0, 0), (0, 1), (1, 0)):
                                ins = pe.matmul(ps, (hh, hl)[a][p][:, c, i * P:(i + 1) * P],
                                                (w2h, w2l)[b_][:, bass.ds(e2 * (FC * D) + c * D, D)],
                                                start=False, stop=(c == FC - 1 and a == 1))
                    ins.then_inc(s["yy_ps"], 1)

            expert_steps(pe, step)


_INS = ['x', 'ctx_1024', 'condB_tau', 'fside_BxS2_0', 'L0_xcond_Wq', 'L0_xcond_bq', 'L0_xcond_Wk', 'L0_xcond_bk',
        'L0_xcond_Wv', 'L0_xcond_bv', 'L0_xcond_Wo', 'L0_xcond_bo', 'L0_ffn_W1', 'L0_ffn_b1', 'L0_ffn_W2',
        'L0_ffn_b2', 'L0_ffn_Wr', 'L0_ffn_br']


def kernel(**inputs):
    import numpy as _np
    import concourse.bacc as _bacc
    from concourse import mybir as _mybir
    from concourse.bass_utils import run_bass_kernel_spmd as _run

    nc = _bacc.Bacc("TRN2", target_bir_lowering=False, num_devices=1)
    arrays, args = {}, []
    for name in _INS:
        a = _np.ascontiguousarray(inputs[name])
        arrays[f"in_{name}_dram"] = a
        args.append(nc.dram_tensor(f"in_{name}_dram", a.shape, _mybir.dt.from_np(a.dtype), kind="ExternalInput").ap())
    args.append(nc.dram_tensor("out_dram", (T + P, D), _mybir.dt.float32, kind="ExternalOutput").ap())
    moe_block_kernel(nc, *args)
    r = _run(nc, [arrays], core_ids=[0])
    return r.results[0]["out_dram"][0:T].reshape(B, S, D)
```

```python
import concourse.bass as bass
from concourse import mybir
from contextlib import ExitStack

P = 128
B, S, D = 16, 128, 256
KT = D // P
H, DK = 16, 16
E, F = 8, 1024
FC = F // P
T = B * S
G = B // 2
SMALL = 4
TW = 2 * P
NT = (2 * T - E) // TW + E
NS = 2 * NT
EPS = 1e-5

fp32 = mybir.dt.float32
fp16 = mybir.dt.float16
i32 = mybir.dt.int32
ALU = mybir.AluOpType
ACT = mybir.ActivationFunctionType
AX = mybir.AxisListType


def known(t):
    return isinstance(t, int)


def moe_block_kernel(nc, x, ctx_in, tau, side, Wq, bq, Wk, bk, Wv, bv, Wo, bo,
                     W1, b1, W2, b2, Wr, br, out):
    stack = ExitStack()
    with stack:
        def sb(name, shape, dt=fp32):
            return stack.enter_context(nc.sbuf_tensor(name, shape, dt))

        def sem(name):
            return stack.enter_context(nc.semaphore(name))

        q_dram = nc.dram_tensor("q_dram", (2, H // 4, 2, 3, DK, 4 * S), fp16, kind="Internal").ap()
        k_dram = nc.dram_tensor("k_dram", (2, H // 4, 2, 3, DK, 4 * S), fp16, kind="Internal").ap()
        delta_dram = nc.dram_tensor("delta_dram", (2, B, S), fp16, kind="Internal").ap()
        rows_dram = nc.dram_tensor("rows_dram", (2, E + 4, D), fp16, kind="Internal").ap()
        xn2_dram = nc.dram_tensor("xn2_dram", (T + P, D), fp32, kind="Internal").ap()

        w1h = sb("w1h", [P, E * KT * F], fp16)
        w1l = sb("w1l", [P, E * KT * F], fp16)
        w2h = sb("w2h", [P, E * FC * D], fp16)
        w2l = sb("w2l", [P, E * FC * D], fp16)
        stage = sb("stage", [P, 2, 1024])
        wah = sb("wah", [P, 4, KT, D], fp16)
        wal = sb("wal", [P, 4, KT, D], fp16)
        wr = sb("wr", [P, KT, E])
        brb = sb("brb", [P, E])
        bob = sb("bob", [P, D])
        bcols = sb("bcols", [P, E * FC])
        tau4 = sb("tau4", [P, B])
        qrow = sb("qrow", [3, D], fp16)
        trow = sb("trow", [3, B], fp16)
        kvrow = sb("kvrow", [2, 2, D], fp16)
        ident = sb("ident", [P, P])
        identh = sb("identh", [P, P], fp16)
        onesh = sb("onesh", [P, P], fp16)
        trih = sb("trih", [P, P], fp16)
        sel = sb("sel", [2 * H, H], fp16)
        nhalf = sb("nhalf", [P, 2])
        rev = sb("rev", [P, E])
        steps = sb("steps", [P, B])
        notfirst = sb("notfirst", [P, E * B], fp16)
        tokval = sb("tokval", [P, 2, B], fp16)
        slot_no = sb("slot_no", [P, P], fp16)
        tile_no = sb("tile_no", [P, NS], fp16)
        part_no = sb("part_no", [P, 1])
        xin = sb("xin", [P, 2, D])
        cin = sb("cin", [P, 2, D])
        xn = sb("xn", [P, 2, D])
        xb = sb("xb", [P, 2, 2, D])
        st1 = sb("st1", [P, 2, 6])
        mv1 = sb("mv1", [P, 2, 2])
        rs1 = sb("rs1", [P, 3, 2])
        xT = sb("xT", [P, 4, KT, 2 * S], fp16)
        qkc = sb("qkc", [P, 4, KT, 2 * S], fp16)
        QK = sb("QK", [P, 2, 2, H // 2, 2 * S], fp16)
        V = sb("V", [P, 2, 2, 2, H, DK + 1], fp16)
        PT = sb("PT", [P, 3 * 1024])
        mx = sb("mx", [P, H])
        mm = sb("mm", [P, 2 * H], fp16)
        mT = sb("mT", [2 * H, S], fp16)
        rec = sb("rec", [P, H])
        on = sb("on", [P, H, DK])
        oT = sb("oT", [P, 2, KT, S], fp16)
        x1 = sb("x1", [P, 2, D])
        xn2 = sb("xn2", [P, 2, D])
        st2 = sb("st2", [P, 6])
        mv2 = sb("mv2", [P, 2])
        rs2 = sb("rs2", [P, 2])
        xn2T = sb("xn2T", [P, KT, S])
        sc = sb("sc", [P, E, B])
        rc = sb("rc", [P, 3, E])
        slot_rows = sb("slot_rows", [P, NS], i32)

        QS, KS = QK[:, 0, :, :, :], QK[:, 1, :, :, :]
        flatPT = PT[:, :]
        bias_rows = flatPT[:, 0:P]
        rows32 = flatPT[0:E + 4, 128:384]
        delta = flatPT[0:B, 384:512]
        rparts = flatPT[0:E + 4, 512:768].bitcast(fp16).rearrange("p (r d) -> p r d", r=2)
        dparts = flatPT[0:B, 768:896].bitcast(fp16).rearrange("p (r s) -> p r s", r=2)
        P32 = PT[:, 0:1024].rearrange("p (a n) -> p a n", a=2)
        PH, PL = [PT[:, r * 1024:(r + 1) * 1024].bitcast(fp16).rearrange("p (h n) -> p h n", n=S) for r in (1, 2)]
        flatxb = xb[:, :, :, :].rearrange("p a b d -> p (a b d)")
        hot = flatxb[:, 0:256].rearrange("p (c e b) -> p c e b", c=2, e=E)
        ra = flatxb[:, 256:640].rearrange("p (c e b) -> p c e b", c=3, e=E)
        rb = flatxb[:, 640:768].rearrange("p (c b) -> p c b", b=B)
        tile_e = xn[0:1, :, :].rearrange("p a d -> p (a d)")[:, 0:NT * E].rearrange("p (j e) -> p j e", e=E)
        flatQK = QK[:, :, :, :, :].rearrange("p q a b c -> p (q a b c)")
        hot_tile = flatQK[:, 0:2 * B * NS].rearrange("p (i j) -> p i j", j=NS)
        b2r = V[0:2, :, :, :, :, :].rearrange("p r a b h d -> p (r a b h d)")[:, 0:E * D]
        hot_slot = flatPT[:, 0:2048].bitcast(fp16)\
            .rearrange("p (i r) -> p i r", r=P)
        hot_val = flatQK[:, 2 * B * NS:2 * B * 4 * NS].rearrange("p (i v j) -> p i v j", v=3, j=NS)
        flatqk = qkc[:, :, :, :].rearrange("p a k n -> p (a k n)")
        mask = flatqk[:, 0:128]
        pos = flatqk[:, 128:192].bitcast(fp32).rearrange("p (c b) -> p c b", c=2)
        posi = flatqk[:, 192:384].bitcast(i32).rearrange("p (c b) -> p c b", c=3)
        posf = flatqk[:, 384:448].rearrange("p (c b) -> p c b", c=2)
        vals = flatqk[:, 448:544].rearrange("p (c b) -> p c b", c=3)
        slot_t = flatqk[:, 544:544 + 4 * NS].bitcast(fp32).rearrange("p (c j) -> p c j", c=2)
        slot_w = flatqk[:, 896:896 + 2 * NS].bitcast(fp32)
        tile_f = flatqk[0:1, 768:768 + 2 * NT].bitcast(fp32)
        tile_exp = qrow[0:1, 0:2 * NT].bitcast(i32)
        idxg, idxs = wr[:, 0, 0:4].bitcast(i32), wr[:, 0, 4:6].bitcast(i32)
        xs = (xin, cin)
        hid = [PT[:, u * 512:(u + 1) * 512] for u in range(4)]
        hh, hl = [[flatQK[:, (2 * a + r) * 2048:(2 * a + r + 1) * 2048].rearrange("p (c n) -> p c n", n=TW)
                   for r in range(2)] for a in range(2)]
        yw = (x1, xn2)

        banks = [stack.enter_context(nc.psum_tensor(f"bank{i}", [P, 512], fp32)) for i in range(8)]
        psS, psST, pA, pB = banks[0:2], banks[2:4], banks[4], banks[5]
        pT6 = banks[6][:, 0:256].rearrange("p (k n) -> p k n", k=KT)
        pY6 = banks[6][:, 256:512]
        pO = banks[7][:, 0:H * (DK + 1)].rearrange("p (h d) -> p h d", d=DK + 1)
        pM = banks[7][:, 288:352].bitcast(fp16)
        pR = pY6[:, 0:E]

        names = """zeroed const_ready ones_ready bcols_loaded wa_loaded small_in
            wT_ps wT_hi wT_lo bc_ps bc_ready delta_split delta_stored rows_split rows_stored rows_in
            tau_ready tau_in rows32_in ident_ready b2_moved zeros_stored w_hi w_lo
            ln1_stats rstd1 xb_ready xn_ready xT_ps cT_ps xh_ready ch_ready xl_ready cl_ready q_ps k_ps
            qh_ready kh_ready ql_ready kl_ready v_ps vh_ready vl_ready q_stored k_stored
            s_ps m_red mm_ready mT_ps mT_ready st_ps exp_done pv_used po_ps on_ready oT_ps oh_ready ol_ready
            y_ps x1_ready ln2_stats rstd2 xn2_ready x2T_ps x2T_ready r_ps sc_ready
            c_setup c_pool c_ln1 c_rs1 c_mm c_on c_ln2 c_rs2 c_route
            mask_ready gap_ready e_ready rank_ps hot_ready slot_ps routed
            idxg_ready idxs_ready gT_ps gh_ready gl_ready h_ps gelu_done hh_done hl_done yy_ps yy_ready
            added""".split()
        s = {n: sem(n) for n in names}
        x_loaded, c_loaded = sem("x_loaded"), sem("c_loaded")
        stack_ready = [sem(f"stack_ready{i}") for i in range(2)]
        x1_stored = [sem(f"x1_stored{i}") for i in range(2)]
        xn2_stored = [sem(f"xn2_stored{i}") for i in range(2)]
        pl_ready = [sem(f"pl_ready{i}") for i in range(4)]
        w_loaded = [sem(f"w_loaded{i}") for i in range(2)]
        rows_in = [sem(f"rows_in{i}") for i in range(2)]
        block = stack.enter_context(nc.Block())

        def wait(eng, name, n):
            if not known(n) or n > 0:
                eng.wait_ge(s[name] if isinstance(name, str) else name, n)

        def own_wait(eng, name, n):
            if known(n):
                eng.wait_ge(s[name], n)
            else:
                n = eng.to_reg(n)
                eng.wait_ge(s["const_ready"], 1)
                eng.wait_ge(s[name], n)

        def chain(eng, name, base=0):
            k = [0]

            def link(ins):
                k[0] += 1
                ins.then_inc(s[name], 1)
                eng.wait_ge(s[name], base + k[0])
            return link

        def attention_steps(eng, step):
            for t in range(3):
                step(t, t % 2)
            with eng.Fori(1, 3) as i:
                step(i * 2 + 1, 1)
                step(i * 2 + 2, 0)
            for t in range(G - 1, G + 2):
                step(t, t % 2)

        def batch_in(t, bb, late):
            return not known(t) or 0 <= 2 * t - 2 + bb - late < B

        def expert_steps(eng, step):
            for t in range(4):
                step(t, t % 2)
            with eng.Fori(2, (NT - 2) // 2) as i:
                step(i * 2, 0)
                step(i * 2 + 1, 1)
            for t in range((NT - 2) // 2 * 2, NT + 2):
                step(t, t % 2)

        def has(t, lo, hi):
            return not known(t) or lo <= t < hi

        ROWS = 3 * DK + 2

        def head_of(place):
            u, j = place // 4, 4 * (place // 8) + place % 4
            return 8 * (j % 2) + 2 * (j // 2) + u % 2

        @block.sync
        def _(sp):
            def load_x(g):
                wait(sp, "xn_ready", g)
                own_wait(sp, "xb_ready", g)
                sp.dma_start(xin[:, :, :], x[bass.ds(g * 2, 2), :, :].rearrange("b s d -> s b d"))\
                  .then_inc(x_loaded, 16)

            def load_ctx(g):
                own_wait(sp, "cT_ps", g)
                sp.dma_start(cin[:, :, :], ctx_in[bass.ds(g * 2, 2), :, :].rearrange("b s d -> s b d"))\
                  .then_inc(c_loaded, 16)

            def load_w(e, n):
                (own_wait if not known(e) else wait)(sp, "w_lo", 4 * e + n - 1)
                if n < 2:
                    src = W1[bass.ds(e, 1), n * P:(n + 1) * P, :].rearrange("e p n -> p (e n)")
                    dst = stage[:, n % 2, :]
                else:
                    src = W2[bass.ds(e, 1), (n - 2) * 512:(n - 1) * 512, :]\
                        .rearrange("e (c p) d -> p (e c) d", p=P)
                    dst = stage[:, n % 2, :].rearrange("p (c d) -> p c d", d=D)
                sp.dma_start(dst, src).then_inc(w_loaded[n % 2], 16)

            def rows(v):
                return v.rearrange("(a n) -> a n", a=1)

            load_x(0)
            sp.dma_start(tau4[:, :], rows(tau).to_broadcast([P, B])).then_inc(s["tau_in"], 16)
            sp.wait_ge(s["zeroed"], 1)
            sp.dma_start(rows32[0:E, :], b2).then_inc(s["rows32_in"], 16)
            for r, v in enumerate((bq, bk, bv)):
                sp.dma_start(rows32[E + r:E + r + 1, :], rows(v)).then_inc(s["rows32_in"], 16)
            sp.dma_start(rows32[E + 3:E + 4, 0:B], rows(tau)).then_inc(s["rows32_in"], 16)
            for n, w in enumerate((Wq, Wk, Wv, Wo)):
                sp.dma_start(stage[:, n // 2, (n % 2) * 512:(n % 2 + 1) * 512].rearrange("p (a i) -> p a i", i=D),
                             w.rearrange("(a p) i -> p a i", p=P)).then_inc(s["wa_loaded"], 16)
            load_ctx(0)
            sp.dma_start(bias_rows[0:64, :], b1.rearrange("e (c p) -> (e c) p", p=P)).then_inc(s["bcols_loaded"], 16)
            sp.wait_ge(s["rows_split"], 1)
            for r in range(2):
                sp.dma_start(rows_dram[r], rparts[:, r, :]).then_inc(s["rows_stored"], 16)
            sp.dma_start(delta, side).then_inc(s["small_in"], 16)
            sp.dma_start(bob[:, :], rows(bo).to_broadcast([P, D])).then_inc(s["small_in"], 16)
            sp.dma_start(wr[:, :, :], Wr.rearrange("(k p) e -> p k e", p=P)).then_inc(s["small_in"], 16)
            sp.dma_start(brb[:, :], rows(br).to_broadcast([P, E])).then_inc(s["small_in"], 16)
            sp.wait_ge(s["rows_stored"], 32)
            sp.dma_start(qrow[0:2, :], rows_dram[0:1, E, :].to_broadcast([2, D])).then_inc(s["rows_in"], 16)
            sp.dma_start(qrow[2:3, :], rows_dram[1:2, E, :]).then_inc(s["rows_in"], 16)
            sp.dma_start(trow[0:2, :], rows_dram[:, E + 3, 0:B]).then_inc(s["rows_in"], 16)
            sp.dma_start(trow[2:3, :], rows_dram[0:1, E + 3, 0:B]).then_inc(s["rows_in"], 16)
            sp.dma_start(kvrow[:, :, :], rows_dram[:, E + 1:E + 3, :]).then_inc(s["rows_in"], 16)
            sp.wait_ge(s["delta_split"], 1)
            for r in range(2):
                sp.dma_start(delta_dram[r], dparts[:, r, :]).then_inc(s["delta_stored"], 16)
            sp.dma_start(xn2_dram[T:T + P, :], xn2[:, 0, :]).then_inc(s["zeros_stored"], 16)
            sp.dma_start(out[T:T + P, :], xn2[:, 0, :]).then_inc(s["zeros_stored"], 16)
            sp.wait_ge(s["delta_stored"], 32)
            sp.wait_ge(s["wT_ps"], 4)
            load_w(0, 0)
            load_w(0, 1)

            def put_x1(b, bb):
                sp.wait_ge(s["x1_ready"], b + 1)
                sp.dma_start(out[bass.ds(b * S, S), :], x1[:, bb, :]).then_inc(x1_stored[bb], 16)

            def put_xn2(b, bb):
                sp.wait_ge(s["xn2_ready"], b + 1)
                sp.dma_start(xn2_dram[bass.ds(b * S, S), :], xn2[:, bb, :]).then_inc(xn2_stored[bb], 16)

            def store_parts(dram, p, parts, name):
                for r, n in enumerate(parts):
                    sp.dma_start(dram[p, :, :, r].rearrange("j a i n -> (j a) i n"),
                                 qkc[:, n, :, :].rearrange("p k n -> p (k n)")).then_inc(s[name], 16)

            def load_stacks(dst, dram, p):
                for par in range(2):
                    sp.dma_start(dst[64 * par:64 * par + 3 * DK, p, :, :].rearrange("p (j c) n -> p j (c n)", c=2),
                                 dram[p, :, par].rearrange("j r i n -> (r i) j n")).then_inc(stack_ready[p], 16)

            def load_deltas(t, p):
                wait(sp, "st_ps", 8 * (t - 1))
                for par in range(2):
                    r = 64 * par + 3 * DK
                    src = delta_dram[:, bass.ds(t * 2, 2), :].rearrange("r b n -> r (b n)")
                    sp.dma_start(KS[r:r + 2, p, :, :],
                                 src.unsqueeze(1).to_broadcast([2, H // 2, 2 * S]))\
                      .then_inc(stack_ready[p], 16)

            def store_k(g, p):
                sp.wait_ge(s["kl_ready"], g + 1)
                store_parts(k_dram, p, (2, 3, 2), "k_stored")

            def step(t, p):
                if known(t) and t == 0:
                    store_k(t, p)
                if has(t, 0, G - 1):
                    load_ctx(t + 1)
                if has(t, 0, G):
                    load_deltas(t, p)
                    own_wait(sp, "k_stored", 48 * (t + 1))
                    load_stacks(KS, k_dram, p)
                if has(t, 1, E):
                    load_w(t, 1)
                if batch_in(t, 0, 2):
                    put_xn2(2 * t - 4, 0)
                if has(t, 0, G):
                    sp.wait_ge(s["ql_ready"], t + 1)
                    store_parts(q_dram, p, (0, 0, 1), "q_stored")
                    sp.wait_ge(s["ones_ready"], 1)
                    own_wait(sp, "q_stored", 48 * (t + 1))
                    load_stacks(QS, q_dram, p)
                if batch_in(t, 0, 1):
                    put_x1(2 * t - 3, 1)
                if has(t, 0, G - 1):
                    load_x(t + 1)
                if has(t, 0, E):
                    load_w(t, 2)
                if batch_in(t, 1, 2):
                    put_xn2(2 * t - 3, 1)
                if has(t, 0, E):
                    load_w(t, 3)
                if batch_in(t, 1, 1):
                    put_x1(2 * t - 2, 0)
                if has(t, 0, G - 1):
                    store_k(t + 1, 1 - p)
                if has(t, 0, E - 1):
                    load_w(t + 1, 0)

            attention_steps(sp, step)
            sp.wait_ge(s["po_ps"], B)
            sp.dma_start(b2r, rows_dram[:, 0:E, :].rearrange("r e d -> r (e d)")).then_inc(s["b2_moved"], 16)

        @block.gpsimd
        def _(pool):
            link = chain(pool, "c_pool")

            def rstd_1(g):
                link = chain(pool, "c_rs1", g)
                own_wait(pool, "ln1_stats", g + 1)
                link(pool.tensor_scalar(rs1[:, 0, :], mv1[:, :, 1], EPS, None, ALU.add))
                pool.tensor_tensor(rs1[:, 1, :], rs1[:, 0, :], nhalf[:, :], ALU.pow).then_inc(s["rstd1"], 1)

            pool.memset(nhalf[:, :], -0.5)
            pool.memset(ident[:, :], 0.0)
            link(pool.memset(identh[:, :], 0.0))
            for m in (ident, identh):
                ins = pool.affine_select(out=m[:, :], in_=m[:, :], compare_op=ALU.not_equal, fill=1.0,
                                         base=0, pattern=[[-1, P]], channel_multiplier=1)
            ins.then_inc(s["ident_ready"], 1)
            rstd_1(0)
            pool.memset(trih[:, :], 0.0)
            pool.memset(sel[:, :], 0.0)
            pool.memset(onesh[:, :], 1.0)
            pool.memset(QS, 1.0).then_inc(s["ones_ready"], 1)
            link(pool.memset(notfirst[:, :], 1.0))
            link(pool.affine_select(out=trih[:, :], in_=trih[:, :], compare_op=ALU.is_ge, fill=1.0,
                                    base=0, pattern=[[-1, P]], channel_multiplier=1))
            for base in (0, -H):
                link(pool.affine_select(out=sel[:, :], in_=sel[:, :], compare_op=ALU.not_equal,
                                        fill=1.0, base=base, pattern=[[-1, H]],
                                        channel_multiplier=1))
            link(pool.affine_select(out=notfirst[:, :], in_=notfirst[:, :], compare_op=ALU.not_equal,
                                    fill=0.0, base=0, pattern=[[0, E], [1, B]], channel_multiplier=0))

            def iota(dst, pattern, base, mult):
                return pool.iota(dst, pattern, base=base, channel_multiplier=mult,
                                 allow_small_or_imprecise_dtypes=True)

            iota(rev[:, :], [[-1, E]], E, 0)
            iota(steps[:, :], [[TW, B]], 0, 0)
            iota(tokval[:, :, :], [[0, 2], [S, B]], -T, 1)
            iota(slot_no[:, :], [[1, P]], 0, 0)
            iota(tile_no[:, :], [[1, NS]], 0, 0)
            iota(part_no[:, :], [[0, 1]], 0, 1).then_inc(s["const_ready"], 1)

            def piece_lo(e, n):
                h, l = ((w1h, w1l), (w2h, w2l))[n // 2]
                at = bass.ds(e * (KT * F) + (n % 2) * 1024, 1024)
                own_wait(pool, "w_hi", 4 * e + n + 1)
                pool.tensor_tensor(l[:, at], stage[:, n % 2, :], h[:, at], ALU.subtract).then_inc(s["w_lo"], 1)

            def x_plus_bo(g, p):
                pool.wait_ge(x_loaded, 16 * (g + 1))
                wait(pool, "x1_ready", 2 * g - 2)
                pool.tensor_tensor(xb[:, p, :, :], xin[:, :, :],
                                   bob[:, :].unsqueeze(1).to_broadcast([P, 2, D]), ALU.add)\
                    .then_inc(s["xb_ready"], 1)

            def exp_lo(b, u):
                pool.wait_ge(s["exp_done"], 4 * b + u + 1)
                pool.tensor_tensor(PL[:, 4 * u:4 * u + 4, :].rearrange("p h n -> p (h n)"), P32[:, u % 2, :],
                                   PH[:, 4 * u:4 * u + 4, :].rearrange("p h n -> p (h n)"), ALU.subtract)\
                    .then_inc(pl_ready[u], 1)

            def rstd_2(b):
                link = chain(pool, "c_rs2", b)
                own_wait(pool, "ln2_stats", b + 1)
                link(pool.tensor_scalar(rs2[:, 0:1], mv2[:, 1:2], EPS, None, ALU.add))
                pool.tensor_tensor(rs2[:, 1:2], rs2[:, 0:1], nhalf[:, 0:1], ALU.pow).then_inc(s["rstd2"], 1)


            pool.wait_ge(s["small_in"], 16 * SMALL)

            def step(t, p):
                for bb in range(2):
                    b = 2 * t - 2 + bb
                    if bb == 0:
                        if batch_in(t, bb, 0):
                            exp_lo(b, 0)
                        if has(t, 0, G):
                            x_plus_bo(t, p)
                        if has(t, 0, E):
                            piece_lo(t, 0)
                        if batch_in(t, bb, 1):
                            rstd_2(b - 1)
                        if has(t, 0, E):
                            piece_lo(t, 1)
                    else:
                        if batch_in(t, bb, 0):
                            exp_lo(b, 0)
                        if has(t, 0, G - 1):
                            rstd_1(t + 1)
                        if has(t, 0, E):
                            piece_lo(t, 2)
                        if batch_in(t, bb, 1):
                            rstd_2(b - 1)
                        if has(t, 0, E):
                            piece_lo(t, 3)

            attention_steps(pool, step)

            pool.wait_ge(s["routed"], 1)
            pool.wait_ge(s["zeros_stored"], 32)
            for i in range(2):
                pool.wait_ge(x1_stored[i], 16 * G)
                pool.wait_ge(xn2_stored[i], 16 * G)

            def gather(j, p):
                wait(pool, "gT_ps", j - 1)
                pool.tensor_copy(idxg[:, 2 * p:2 * p + 2], slot_rows[:, bass.ds(j * 2, 2)]).then_inc(s["idxg_ready"], 1)
                own_wait(pool, "idxg_ready", j + 1)
                for i in range(2):
                    pool.indirect_dma_start(out=xs[p][:, i, :], out_offset=None, in_=xn2_dram,
                                            in_offset=bass.IndirectOffsetOnAxis(ap=idxg[:, 2 * p + i:2 * p + i + 1], axis=0))\
                        .then_inc(rows_in[p], 16)

            def scatter(j, p):
                pool.wait_ge(s["yy_ready"], j + 1)
                wait(pool, "added", 32 * j)
                pool.tensor_copy(idxs, slot_rows[:, bass.ds(j * 2, 2)]).then_inc(s["idxs_ready"], 1)
                own_wait(pool, "idxs_ready", j + 1)
                for i in range(2):
                    if i:
                        own_wait(pool, "added", 32 * j + 16)
                    pool.indirect_dma_start(out=out, out_offset=bass.IndirectOffsetOnAxis(ap=idxs[:, i:i + 1], axis=0),
                                            in_=yw[p][:, i, :], in_offset=None, compute_op=ALU.add)\
                        .then_inc(s["added"], 16)

            gather(0, 0)
            gather(1, 1)

            def step(t, p):
                if has(t, 0, NT - 2):
                    gather(t + 2, p)
                if has(t, 2, NT + 2):
                    scatter(t - 2, p)

            expert_steps(pool, step)
            pool.wait_ge(s["added"], 32 * NT)

        @block.scalar
        def _(act):
            def copy(dst, src):
                return act.activation(dst, src, ACT.Copy)

            for n in range(4):
                act.wait_ge(s["wT_ps"], n + 1)
                copy(wah[:, n, :, :], banks[n][:, :].rearrange("p (k n) -> p k n", k=KT)).then_inc(s["wT_hi"], 1)
            act.wait_ge(s["bc_ps"], 1)
            copy(bcols[:, :], pA[:, 0:E * FC]).then_inc(s["bc_ready"], 1)

            def piece_hi(e, n):
                at = bass.ds(e * (KT * F) + (n % 2) * 1024, 1024)
                act.wait_ge(w_loaded[n % 2], 32 * e + 16 * (n // 2 + 1))
                copy((w1h, w2h)[n // 2][:, at], stage[:, n % 2, :]).then_inc(s["w_hi"], 1)

            def x_hi(g):
                act.wait_ge(s["xT_ps"], g + 1)
                copy(xT[:, 0, :, :], pA[:, :].rearrange("p (k n) -> p k n", k=KT)).then_inc(s["xh_ready"], 1)

            def ctx_hi(g):
                act.wait_ge(s["cT_ps"], g + 1)
                copy(xT[:, 2, :, :], pB[:, :].rearrange("p (k n) -> p k n", k=KT)).then_inc(s["ch_ready"], 1)

            def qk_hi(g, n, ps, name):
                act.wait_ge(s[name + "_ps"], g + 1)
                wait(act, name + "_stored", 48 * g)
                copy(qkc[:, n, :, :], ps[:, :].rearrange("p (k n) -> p k n", k=KT)).then_inc(s[name + "h_ready"], 1)

            def v_hi(g, p):
                act.wait_ge(s["v_ps"], g + 1)
                wait(act, "po_ps", 2 * (g - 1))
                copy(V[:, 0, p, :, :, 0:DK], pA[:, :].rearrange("p (b h d) -> p b h d", b=2, d=DK))\
                    .then_inc(s["vh_ready"], 1)

            def exps(b, u):
                if u in (0, 3):
                    wait(act, ("pv_used", "po_ps")[u // 3], b)
                wait(act, pl_ready[(u + 2) % 4], b + u // 2)
                act.wait_ge(s["st_ps"], 4 * b + u + 1)
                act.activation(P32[:, u % 2, :], psST[u % 2][:, :], ACT.Exp)
                act.activation(PH[:, 4 * u:4 * u + 4, :], psST[u % 2][:, :].rearrange("p (h n) -> p h n", h=4), ACT.Exp)\
                    .then_inc(s["exp_done"], 1)

            def oT_hi(b):
                act.wait_ge(s["oT_ps"], b + 1)
                copy(oT[:, 0, :, :], pT6).then_inc(s["oh_ready"], 1)

            def xn2_T(b):
                act.wait_ge(s["x2T_ps"], b + 1)
                copy(xn2T[:, :, :], pT6).then_inc(s["x2T_ready"], 1)

            def step(t, p):
                for bb in range(2):
                    b = 2 * t - 2 + bb
                    new, att = has(t, 0, G), batch_in(t, bb, 0)
                    if bb == 0:
                        if att:
                            act.wait_ge(s["mT_ps"], b + 1)
                            copy(mT[:, :], pM[0:2 * H, :]).then_inc(s["mT_ready"], 1)
                        if new:
                            x_hi(t)
                        if att:
                            exps(b, 0)
                        if new and known(t) and t == 0:
                            ctx_hi(t)
                        if att:
                            exps(b, 1)
                        if batch_in(t, bb, 1):
                            oT_hi(b - 1)
                        if att:
                            exps(b, 2)
                        if new:
                            qk_hi(t, 0, pA, "q")
                        if new and known(t) and t == 0:
                            qk_hi(t, 2, pB, "k")
                        if new:
                            piece_hi(t, 0)
                        if att:
                            exps(b, 3)
                        if batch_in(t, bb, 2):
                            xn2_T(b - 2)
                        if new:
                            piece_hi(t, 1)
                    else:
                        if att:
                            act.wait_ge(s["mT_ps"], b + 1)
                            copy(mT[:, :], pM[0:2 * H, :]).then_inc(s["mT_ready"], 1)
                            exps(b, 0)
                            exps(b, 1)
                        if batch_in(t, bb, 1):
                            oT_hi(b - 1)
                        if new:
                            v_hi(t, p)
                        if att:
                            exps(b, 2)
                        if has(t, 0, G - 1):
                            ctx_hi(t + 1)
                        if new:
                            piece_hi(t, 2)
                        if att:
                            exps(b, 3)
                        if has(t, 0, G - 1):
                            qk_hi(t + 1, 2, pB, "k")
                        if batch_in(t, bb, 2):
                            xn2_T(b - 2)
                        if new:
                            piece_hi(t, 3)

            attention_steps(act, step)

            act.wait_ge(s["gap_ready"], 1)
            act.activation(rb[:, 5, :], rb[:, 4, :], ACT.Exp).then_inc(s["e_ready"], 1)
            act.wait_ge(s["routed"], 1)

            def step(t, p):
                if has(t, 0, NT):
                    act.wait_ge(s["gT_ps"], t + 1)
                    copy(xT[:, 2 * p, :, :], (pA, pB)[p][:, :].rearrange("p (k n) -> p k n", k=KT))\
                        .then_inc(s["gh_ready"], 1)
                if has(t, 1, NT + 1):
                    j = t - 1
                    e = act.value_load(tile_exp[0:1, bass.ds(j, 1)], min_val=0, max_val=E - 1)
                    for u in range(4):
                        wait(act, "hl_done", 4 * j + u - 3)
                        act.wait_ge(s["h_ps"], 4 * j + u + 1)
                        for c in range(2):
                            ins = act.activation(hid[u][:, c * TW:(c + 1) * TW], banks[u][:, c * TW:(c + 1) * TW],
                                                 ACT.Gelu_apprx_tanh, bias=bcols[:, bass.ds(e * FC + 2 * u + c, 1)])
                        ins.then_inc(s["gelu_done"], 1)

            expert_steps(act, step)

        @block.vector
        def _(dve):
            link = chain(dve, "c_setup")
            dve.memset(rows32, 0.0)
            dve.memset(xn2[:, 0, :], 0.0).then_inc(s["zeroed"], 1)
            dve.memset(V[:, 0, :, :, :, DK], 1.0)
            dve.memset(V[:, 1, :, :, :, DK], 0.0)
            def ln_1_stats(g):
                dve.wait_ge(x_loaded, 16 * (g + 1))
                for i in range(2):
                    ins = dve.bn_stats(st1[:, i, :], xin[:, i, :])
                ins.then_inc(s["c_ln1"], 1)
                own_wait(dve, "c_ln1", 2 * g + 1)
                for i in range(2):
                    ins = dve.bn_aggr(mv1[:, i, :], st1[:, i, :])
                ins.then_inc(s["ln1_stats"], 1)

            def ln_1(g):
                dve.wait_ge(s["rstd1"], g + 1)
                dve.tensor_tensor(rs1[:, 2, :], rs1[:, 1, :], tau4[:, bass.ds(g * 2, 2)], ALU.mult)\
                    .then_inc(s["c_ln1"], 1)
                dve.wait_ge(s["c_ln1"], 2 * g + 2)
                wait(dve, "xT_ps", g)
                for i in range(2):
                    ins = dve.tensor_scalar(xn[:, i, :], xin[:, i, :], mv1[:, i, 0:1], rs1[:, 2, i:i + 1],
                                            ALU.subtract, ALU.mult)
                ins.then_inc(s["xn_ready"], 1)

            def k2(v):
                return v.rearrange("p (k n) -> p k n", k=KT)

            dve.wait_ge(s["tau_in"], 16)
            link(dve.tensor_scalar(tau4[:, :], tau4[:, :], DK ** -0.5, None, ALU.mult))
            ln_1_stats(0)
            dve.wait_ge(s["rows32_in"], 16 * 5)
            link(dve.tensor_copy(rparts[:, 0, :], rows32))
            dve.tensor_tensor(rparts[:, 1, :], rows32, rparts[:, 0, :], ALU.subtract)\
                .then_inc(s["rows_split"], 1)
            ln_1(0)
            dve.wait_ge(s["small_in"], 16 * SMALL)
            link(dve.tensor_scalar(delta, delta, DK ** -0.5, None, ALU.mult))
            link(dve.tensor_copy(dparts[:, 0, :], delta))
            dve.tensor_tensor(dparts[:, 1, :], delta, dparts[:, 0, :], ALU.subtract)\
                .then_inc(s["delta_split"], 1)
            for n in range(4):
                dve.wait_ge(s["wT_hi"], n + 1)
                dve.tensor_tensor(wal[:, n, :, :], k2(banks[n][:, :]), wah[:, n, :, :], ALU.subtract)\
                    .then_inc(s["wT_lo"], 1)
            dve.wait_ge(s["rows_in"], 16 * 5)
            dve.tensor_scalar(trow[:, :], trow[:, :], DK ** -0.5, None, ALU.mult).then_inc(s["tau_ready"], 1)
            dve.wait_ge(s["zeros_stored"], 32)

            def x_lo(g):
                dve.wait_ge(s["xh_ready"], g + 1)
                dve.tensor_tensor(xT[:, 1, :, :], k2(pA[:, :]), xT[:, 0, :, :], ALU.subtract)\
                    .then_inc(s["xl_ready"], 1)

            def ctx_lo(g):
                dve.wait_ge(s["ch_ready"], g + 1)
                dve.tensor_tensor(xT[:, 3, :, :], k2(pB[:, :]), xT[:, 2, :, :], ALU.subtract)\
                    .then_inc(s["cl_ready"], 1)

            def qk_lo(g, n, ps, name):
                dve.wait_ge(s[name + "h_ready"], g + 1)
                dve.tensor_tensor(qkc[:, n + 1, :, :], k2(ps[:, :]), qkc[:, n, :, :], ALU.subtract)\
                    .then_inc(s[name + "l_ready"], 1)

            def v_lo(g, p):
                dve.wait_ge(s["vh_ready"], g + 1)
                dve.tensor_tensor(V[:, 1, p, :, :, 0:DK], pA[:, :].rearrange("p (b h d) -> p b h d", b=2, d=DK),
                                  V[:, 0, p, :, :, 0:DK], ALU.subtract).then_inc(s["vl_ready"], 1)

            def maxima(b, u):
                dve.wait_ge(s["s_ps"], 4 * b + u + 1)
                dve.reduce_max(mx[:, 4 * u:4 * u + 4], psS[u % 2][:, :].rearrange("p (h n) -> p h n", h=4),
                               AX.X).then_inc(s["m_red"], 1)

            def maxima_out(b):
                dve.wait_ge(s["m_red"], 4 * b + 4)
                wait(dve, "mT_ps", b)
                dve.tensor_scalar(mm[:, 0:H], mx[:, :], -1.0, None, ALU.mult).then_inc(s["c_mm"], 1)
                dve.wait_ge(s["c_mm"], b + 1)
                dve.scalar_tensor_tensor(out=mm[:, H:2 * H], in0=mx[:, :], scalar=-1.0, in1=mm[:, 0:H],
                                         op0=ALU.mult, op1=ALU.subtract).then_inc(s["mm_ready"], 1)

            def exp_lo(b, u):
                dve.wait_ge(s["exp_done"], 4 * b + u + 1)
                dve.tensor_tensor(PL[:, 4 * u:4 * u + 4, :].rearrange("p h n -> p (h n)"), P32[:, u % 2, :],
                                  PH[:, 4 * u:4 * u + 4, :].rearrange("p h n -> p (h n)"), ALU.subtract)\
                    .then_inc(pl_ready[u], 1)

            def heads_out(b):
                dve.wait_ge(s["po_ps"], b + 1)
                dve.reciprocal(rec[:, :], pO[:, :, DK]).then_inc(s["c_on"], 1)
                dve.wait_ge(s["c_on"], b + 1)
                wait(dve, "oT_ps", b)
                dve.tensor_tensor(on[:, :, :], pO[:, :, 0:DK], rec[:, :].unsqueeze(2).to_broadcast([P, H, DK]),
                                  ALU.mult).then_inc(s["on_ready"], 1)

            def oT_lo(b):
                dve.wait_ge(s["oh_ready"], b + 1)
                dve.tensor_tensor(oT[:, 1, :, :], pT6, oT[:, 0, :, :], ALU.subtract).then_inc(s["ol_ready"], 1)

            def residual(b, bb, p):
                dve.wait_ge(s["y_ps"], b + 1)
                wait(dve, x1_stored[bb], 8 * (b - bb))
                dve.tensor_tensor(x1[:, bb, :], pY6, xb[:, p, bb, :], ALU.add).then_inc(s["x1_ready"], 1)
                dve.wait_ge(s["x1_ready"], b + 1)
                dve.bn_stats(st2[:, :], x1[:, bb, :]).then_inc(s["c_ln2"], 1)
                own_wait(dve, "c_ln2", b + 1)
                dve.bn_aggr(mv2[:, :], st2[:, :]).then_inc(s["ln2_stats"], 1)

            def ln_2(b, bb):
                dve.wait_ge(s["rstd2"], b + 1)
                wait(dve, xn2_stored[bb], 8 * (b - bb))
                dve.tensor_scalar(xn2[:, bb, :], x1[:, bb, :], mv2[:, 0:1], rs2[:, 1:2],
                                  ALU.subtract, ALU.mult).then_inc(s["xn2_ready"], 1)

            def score(b):
                dve.wait_ge(s["r_ps"], b + 1)
                dve.tensor_tensor(sc[:, :, bass.ds(b, 1)], pR.unsqueeze(2), brb[:, :].unsqueeze(2), ALU.add)\
                    .then_inc(s["sc_ready"], 1)

            def step(t, p):
                for bb in range(2):
                    b = 2 * t - 2 + bb
                    new, att, ahead = has(t, 0, G), batch_in(t, bb, 0), batch_in(t, bb, -1)
                    if bb == 0:
                        if batch_in(t, bb, 1):
                            exp_lo(b - 1, 3)
                        if ahead:
                            maxima(b + 1, 0)
                        if new:
                            x_lo(t)
                        if new and known(t) and t == 0:
                            ctx_lo(t)
                        if batch_in(t, bb, 1):
                            heads_out(b - 1)
                        if ahead:
                            maxima(b + 1, 1)
                        if att:
                            exp_lo(b, 1)
                        if batch_in(t, bb, 1):
                            oT_lo(b - 1)
                        if batch_in(t, bb, 2):
                            ln_2(b - 2, bb)
                        if att:
                            exp_lo(b, 2)
                        if new:
                            qk_lo(t, 0, pA, "q")
                        if new and known(t) and t == 0:
                            qk_lo(t, 2, pB, "k")
                        if ahead:
                            maxima(b + 1, 2)
                        if batch_in(t, bb, 1):
                            residual(b - 1, 1 - bb, p if bb == 0 else 1 - p)
                        if ahead:
                            maxima(b + 1, 3)
                            maxima_out(b + 1)
                        if batch_in(t, bb, 2):
                            score(b - 2)
                    else:
                        if batch_in(t, bb, 1):
                            exp_lo(b - 1, 3)
                            heads_out(b - 1)
                        if batch_in(t, bb, 2):
                            ln_2(b - 2, bb)
                        if att:
                            exp_lo(b, 1)
                        if batch_in(t, bb, 1):
                            oT_lo(b - 1)
                        if new:
                            v_lo(t, p)
                        if ahead:
                            maxima(b + 1, 0)
                        if att:
                            exp_lo(b, 2)
                        if has(t, 0, G - 1):
                            ctx_lo(t + 1)
                        if ahead:
                            maxima(b + 1, 1)
                        if has(t, 0, G - 1):
                            ln_1_stats(t + 1)
                        if batch_in(t, bb, 1):
                            residual(b - 1, 1 - bb, p if bb == 0 else 1 - p)
                        if ahead:
                            maxima(b + 1, 2)
                        if has(t, 0, G - 1):
                            ln_1(t + 1)
                        if ahead:
                            maxima(b + 1, 3)
                            maxima_out(b + 1)
                        if has(t, 0, G - 1):
                            qk_lo(t + 1, 2, pB, "k")
                        if batch_in(t, bb, 2):
                            score(b - 2)

            attention_steps(dve, step)
            dve.wait_ge(s["sc_ready"], B)
            dve.wait_ge(s["const_ready"], 1)

            link = chain(dve, "c_route")

            def over_experts(v):
                return v.rearrange("p e b -> p b e")

            def per_batch(v):
                return v.unsqueeze(1).to_broadcast([P, E, B])

            scores = sc[:, :, :]
            for k in range(2):
                best, first = rb[:, k, :], rb[:, 2 + k, :]
                link(dve.reduce_max(best, over_experts(scores), AX.X))
                link(dve.tensor_tensor(ra[:, 0, :, :], scores, per_batch(best), ALU.is_equal))
                link(dve.tensor_tensor(ra[:, 0, :, :], ra[:, 0, :, :], rev[:, :].unsqueeze(2).to_broadcast([P, E, B]),
                                       ALU.mult))
                link(dve.reduce_max(first, over_experts(ra[:, 0, :, :]), AX.X))
                link(dve.tensor_tensor(hot[:, k, :, :], ra[:, 0, :, :], per_batch(first), ALU.is_equal))
                if k == 0:
                    link(dve.scalar_tensor_tensor(out=ra[:, 1, :, :], in0=hot[:, 0, :, :], scalar=-3.0e38,
                                                  in1=scores, op0=ALU.mult, op1=ALU.add))
                    scores = ra[:, 1, :, :]
            dve.tensor_tensor(rb[:, 4, :], rb[:, 1, :], rb[:, 0, :], ALU.subtract).then_inc(s["gap_ready"], 1)
            mask3 = mask[:, :].rearrange("p (e b) -> p e b", e=E)
            dve.tensor_tensor(mask3, hot[:, 0, :, :], hot[:, 1, :, :], ALU.add).then_inc(s["mask_ready"], 1)
            dve.wait_ge(s["e_ready"], 1)
            link(dve.tensor_scalar(rb[:, 6, :], rb[:, 5, :], 1.0, None, ALU.add))
            pw = rb[:, 6:8, :]
            link(dve.reciprocal(rb[:, 6, :], rb[:, 6, :]))
            link(dve.tensor_tensor(rb[:, 7, :], rb[:, 5, :], rb[:, 6, :], ALU.mult))
            link(dve.tensor_copy(vals[:, 1, :].rearrange("p (c b) -> p c b", c=2), pw))
            dve.tensor_copy(vals[:, 0, :].rearrange("p (c b) -> p c b", c=2), tokval[:, :, :])
            link(dve.tensor_tensor(vals[:, 2, :].rearrange("p (c b) -> p c b", c=2), pw,
                                   vals[:, 1, :].rearrange("p (c b) -> p c b", c=2), ALU.subtract))
            ranks, counts = pA[:, 0:P], pA[:, P:2 * P]
            flat = [ra[:, i, :, :].rearrange("p e b -> p (e b)") for i in range(3)]
            dve.wait_ge(s["rank_ps"], 1)
            link(dve.tensor_tensor_scan(flat[0], notfirst[:, :], counts, 0.0, ALU.mult, ALU.add))
            link(dve.tensor_tensor(ra[:, 1, :, :], ra[:, 0, :, B - 1:B].to_broadcast([P, E, B]),
                                   steps[:, :].unsqueeze(1).to_broadcast([P, E, B]), ALU.is_gt))
            link(dve.reduce_sum(rc[:, 0, :], ra[:, 1, :, :], AX.X))
            link(dve.tensor_tensor_scan(rc[:, 1, :], onesh[:, 0:E], rc[:, 0, :], 0.0, ALU.mult, ALU.add))
            link(dve.tensor_tensor(rc[:, 2, :], rc[:, 1, :], rc[:, 0, :], ALU.subtract))
            link(dve.tensor_tensor(flat[0], flat[0], counts, ALU.subtract))
            link(dve.tensor_tensor(flat[0], flat[0], ranks, ALU.add))
            link(dve.scalar_tensor_tensor(out=ra[:, 2, :, :], in0=rc[:, 2, :].unsqueeze(2).to_broadcast([P, E, B]),
                                          scalar=float(TW), in1=ra[:, 0, :, :], op0=ALU.mult, op1=ALU.add))
            for k in range(2):
                link(dve.tensor_tensor(ra[:, k, :, :], hot[:, k, :, :], ra[:, 2, :, :], ALU.mult))
                link(dve.reduce_sum(pos[:, k, :], over_experts(ra[:, k, :, :]), AX.X))
            link(dve.tensor_copy(posi[:, 0, :], pos[:, :, :].rearrange("p c b -> p (c b)")))
            link(dve.tensor_scalar(posi[:, 1, :], posi[:, 0, :], 7, None, ALU.arith_shift_right))
            link(dve.tensor_scalar(posi[:, 2, :], posi[:, 0, :], P - 1, None, ALU.bitwise_and))
            link(dve.tensor_copy(posf[:, :, :], posi[:, 1:3, :]))
            link(dve.tensor_tensor(hot_tile, tile_no[:, :].unsqueeze(1).to_broadcast([P, 2 * B, NS]),
                                   posf[:, 0, :].unsqueeze(2).to_broadcast([P, 2 * B, NS]), ALU.is_equal))
            for v in range(3):
                dve.tensor_tensor(hot_val[:, :, v, :], hot_tile,
                                  vals[:, v, :].unsqueeze(2).to_broadcast([P, 2 * B, NS]), ALU.mult)
            dve.tensor_tensor(hot_slot, slot_no[:, :].unsqueeze(1).to_broadcast([P, 2 * B, P]),
                              posf[:, 1, :].unsqueeze(2).to_broadcast([P, 2 * B, P]), ALU.is_equal)\
                .then_inc(s["hot_ready"], 1)
            link(dve.tensor_tensor(tile_e, rc[0:1, 1, :].unsqueeze(1).to_broadcast([1, NT, E]),
                                   tile_no[0:1, 0:NT].unsqueeze(2).to_broadcast([1, NT, E]), ALU.is_le))
            link(dve.reduce_sum(tile_f, tile_e, AX.X))
            link(dve.tensor_scalar(tile_exp, tile_f, float(E - 1), None, ALU.min))
            dve.wait_ge(s["slot_ps"], 1)
            link(dve.tensor_copy(slot_t[:, :, :], pB[:, 0:2 * NS].rearrange("p (a j) -> p a j", a=2)))
            link(dve.tensor_tensor(slot_w, slot_t[:, 1, :], pB[:, 2 * NS:3 * NS], ALU.add))
            link(dve.tensor_scalar(slot_t[:, 1, :], slot_t[:, 0, :], 0.0, part_no[:, 0:1], ALU.is_equal, ALU.mult))
            dve.scalar_tensor_tensor(out=slot_rows[:, :], in0=slot_t[:, 0, :], scalar=float(T),
                                     in1=slot_t[:, 1, :], op0=ALU.add, op1=ALU.add).then_inc(s["routed"], 1)

            def step(t, p):
                if has(t, 0, NT):
                    dve.wait_ge(s["gh_ready"], t + 1)
                    dve.tensor_tensor(xT[:, 2 * p + 1, :, :], k2((pA, pB)[p][:, :]), xT[:, 2 * p, :, :],
                                      ALU.subtract).then_inc(s["gl_ready"], 1)
                if has(t, 1, NT + 1):
                    j, q = t - 1, 1 - p
                    wait(dve, "yy_ps", j - 1)
                    for u in range(4):
                        dve.wait_ge(s["gelu_done"], 4 * j + u + 1)
                        parts = [v[q][:, 2 * u:2 * u + 2, :].rearrange("p c n -> p (c n)") for v in (hh, hl)]
                        dve.tensor_copy(parts[0], hid[u]).then_inc(s["hh_done"], 1)
                        own_wait(dve, "hh_done", 4 * j + u + 1)
                        dve.tensor_tensor(parts[1], hid[u], parts[0], ALU.subtract).then_inc(s["hl_done"], 1)
                if has(t, 2, NT + 2):
                    j = t - 2
                    dve.wait_ge(s["yy_ps"], j + 1)
                    wait(dve, "added", 32 * (j - 1))
                    for i in range(2):
                        ins = dve.tensor_scalar(yw[p][:, i, :], banks[6 + p][:, i * D:(i + 1) * D],
                                                slot_w[:, bass.ds(j * 2 + i, 1)], None, ALU.mult)
                    ins.then_inc(s["yy_ready"], 1)

            expert_steps(dve, step)

        @block.tensor
        def _(pe):
            def split_product(ps, lhs, rhs, first=True, last=True):
                for k in range(KT):
                    for i, (a, b_) in enumerate(((0, 0), (0, 1), (1, 0))):
                        ins = pe.matmul(ps, lhs(a, k), rhs(b_, k), start=first and k == 0 and i == 0,
                                        stop=last and k == KT - 1 and i == 2)
                return ins

            wa = (wah, wal)
            pe.wait_ge(s["ident_ready"], 1)
            pe.wait_ge(s["wa_loaded"], 64)
            for n in range(4):
                for k in range(KT):
                    for a in range(2):
                        ins = pe.transpose(banks[n][:, k * D + a * P:k * D + (a + 1) * P],
                                           stage[:, n // 2, (n % 2) * 512 + a * D + k * P:(n % 2) * 512 + a * D + (k + 1) * P], ident[:, :])
                ins.then_inc(s["wT_ps"], 1)
            pe.wait_ge(s["bcols_loaded"], 16)
            pe.transpose(pA[:, 0:E * FC], bias_rows[0:E * FC, :], ident[0:E * FC, 0:E * FC]).then_inc(s["bc_ps"], 1)

            def turn_x(g):
                pe.wait_ge(s["xn_ready"], g + 1)
                wait(pe, "vl_ready", g)
                if known(g) and g == 0:
                    pe.wait_ge(s["bc_ready"], 1)
                for k in range(KT):
                    for i in range(2):
                        ins = pe.transpose(pA[:, (2 * k + i) * P:(2 * k + i + 1) * P],
                                           xn[:, i, k * P:(k + 1) * P], ident[:, :])
                ins.then_inc(s["xT_ps"], 1)

            def turn_ctx(g):
                pe.wait_ge(c_loaded, 16 * (g + 1))
                wait(pe, "kl_ready", g)
                for k in range(KT):
                    for i in range(2):
                        ins = pe.transpose(pB[:, (2 * k + i) * P:(2 * k + i + 1) * P],
                                           cin[:, i, k * P:(k + 1) * P], ident[:, :])
                ins.then_inc(s["cT_ps"], 1)

            def project_q(g):
                pe.wait_ge(s["xl_ready"], g + 1)
                for c in range(KT):
                    o = pA[:, c * 2 * S:(c + 1) * 2 * S]
                    split_product(o, lambda a, k: wa[a][:, 0, k, c * P:(c + 1) * P],
                                  lambda a, k: xT[:, a, k, :], last=False)
                    if known(g) and g == 0:
                        pe.wait_ge(s["tau_ready"], 1)
                    ins = pe.matmul(o, qrow[:, c * P:(c + 1) * P],
                                    trow[:, bass.ds(g * 2, 2)].unsqueeze(2).to_broadcast([3, 2, S]),
                                    start=False, stop=True)
                ins.then_inc(s["q_ps"], 1)

            def project_k(g):
                pe.wait_ge(s["cl_ready"], g + 1)
                for c in range(KT):
                    o = pB[:, c * 2 * S:(c + 1) * 2 * S]
                    split_product(o, lambda a, k: wa[a][:, 1, k, c * P:(c + 1) * P],
                                  lambda a, k: xT[:, 2 + a, k, :], last=False)
                    ins = pe.matmul(o, kvrow[:, 0, c * P:(c + 1) * P], onesh[0:2, 0:1].to_broadcast([2, 2 * S]),
                                    start=False, stop=True)
                ins.then_inc(s["k_ps"], 1)

            def project_v(g, i):
                if i == 0:
                    pe.wait_ge(s["ql_ready"], g + 1)
                o = pA[:, i * D:(i + 1) * D]
                split_product(o, lambda a, k: xT[:, 2 + a, k, i * S:(i + 1) * S],
                              lambda a, k: wa[a][:, 2, k, :], last=False)
                ins = pe.matmul(o, onesh[0:2, :], kvrow[:, 1, :], start=False, stop=True)
                if i == 1:
                    ins.then_inc(s["v_ps"], 1)

            def scores(b, bb, p, u, keys_first):
                r = 64 * (u % 2)
                ps = (psST if keys_first else psS)[u % 2]
                wait(pe, "exp_done" if keys_first else "m_red", 4 * b + u - 1)
                for i in range(4):
                    j = 4 * (u // 2) + i
                    q = QS[r:r + ROWS, p, j, bb * S:(bb + 1) * S]
                    k = KS[r:r + ROWS, p, j, bb * S:(bb + 1) * S]
                    o = ps[:, i * S:(i + 1) * S]
                    if keys_first:
                        pe.matmul(o, k, q, start=True, stop=False)
                        ins = pe.matmul(o, sel[:, 4 * u + i:4 * u + i + 1].to_broadcast([2 * H, S]), mT[:, :],
                                        start=False, stop=True)
                    else:
                        ins = pe.matmul(o, q, k, start=True, stop=True)
                ins.then_inc(s["st_ps" if keys_first else "s_ps"], 1)

            def values(b, bb, p, u):
                if u == 0:
                    wait(pe, "on_ready", b)
                pe.wait_ge(pl_ready[u], b + 1)
                for k in range(4 * u, 4 * u + 4):
                    h = head_of(k)
                    for w, r in ((PH, 0), (PH, 1), (PL, 0)):
                        ins = pe.matmul(pO[:, h, :], w[:, k, :], V[:, r, p, bb, h, :],
                                        start=(w is PH and r == 0), stop=(w is PL))
                if u >= 2:
                    ins.then_inc(s[("pv_used", "po_ps")[u - 2]], 1)

            def turn_heads(b):
                pe.wait_ge(s["on_ready"], b + 1)
                wait(pe, "sc_ready", b - 1)
                for k in range(KT):
                    ins = pe.transpose(pT6[:, k, :], on[:, :, :].rearrange("p h d -> p (h d)")[:, k * P:(k + 1) * P],
                                       ident[:, :])
                ins.then_inc(s["oT_ps"], 1)

            def out_product(b):
                pe.wait_ge(s["ol_ready"], b + 1)
                split_product(pY6, lambda a, k: oT[:, a, k, :], lambda a, k: wa[a][:, 3, k, :])\
                    .then_inc(s["y_ps"], 1)

            def turn_xn2(b, bb):
                pe.wait_ge(s["xn2_ready"], b + 1)
                wait(pe, "x1_ready", b + 2 if not known(b) else min(b + 2, B))
                for k in range(KT):
                    ins = pe.transpose(pT6[:, k, :], xn2[:, bb, k * P:(k + 1) * P], ident[:, :])
                ins.then_inc(s["x2T_ps"], 1)

            def route(b):
                pe.wait_ge(s["x2T_ready"], b + 1)
                for k in range(KT):
                    ins = pe.matmul(pR, xn2T[:, k, :], wr[:, k, :], start=(k == 0), stop=(k == KT - 1))
                ins.then_inc(s["r_ps"], 1)

            pe.wait_ge(s["small_in"], 16 * SMALL)
            pe.wait_ge(s["const_ready"], 1)
            pe.wait_ge(s["wT_lo"], 4)

            def stay_warm(ps, n):
                for _ in range(n):
                    pe.matmul(ps[:, :], identh[:, :], wah[:, 0, :, :].rearrange("p k n -> p (k n)"),
                              start=True, stop=True)

            def step(t, p):
                q = 1 - p
                for bb in range(2):
                    b = 2 * t - 2 + bb
                    new, att, ahead = has(t, 0, G), batch_in(t, bb, 0), batch_in(t, bb, -1)
                    if bb == 0:
                        if att:
                            pe.wait_ge(s["mm_ready"], b + 1)
                            pe.transpose(pM[0:2 * H, :], mm[:, :], identh[:, :]).then_inc(s["mT_ps"], 1)
                        if ahead:
                            scores(b + 1, 1, q, 0, False)
                        if new:
                            turn_x(t)
                        if new and known(t) and t == 0:
                            turn_ctx(t)
                        if att:
                            pe.wait_ge(s["mT_ready"], b + 1)
                            scores(b, 0, q, 0, True)
                            scores(b, 0, q, 1, True)
                        if batch_in(t, bb, 1):
                            values(b - 1, 1, p, 3)
                        if ahead:
                            scores(b + 1, 1, q, 1, False)
                        if att:
                            scores(b, 0, q, 2, True)
                        if batch_in(t, bb, 1):
                            turn_heads(b - 1)
                        if new:
                            project_q(t)
                        if new and known(t) and t == 0:
                            project_k(t)
                        if att:
                            scores(b, 0, q, 3, True)
                            pe.wait_ge(s["vl_ready"], t)
                            values(b, 0, q, 0)
                        if ahead:
                            scores(b + 1, 1, q, 2, False)
                        if batch_in(t, bb, 1):
                            out_product(b - 1)
                        if att:
                            values(b, 0, q, 1)
                        if att:
                            pe.wait_ge(s["exp_done"], 4 * b + 3)
                            stay_warm(psST[0], 1)
                        if ahead:
                            scores(b + 1, 1, q, 3, False)
                        if batch_in(t, bb, 2):
                            turn_xn2(b - 2, 0)
                        if att:
                            values(b, 0, q, 2)
                            stay_warm(psST[0], 2)
                        if batch_in(t, bb, 2):
                            route(b - 2)
                        if att:
                            stay_warm(psST[0], 3)
                    else:
                        if att:
                            pe.wait_ge(s["mm_ready"], b + 1)
                            pe.transpose(pM[0:2 * H, :], mm[:, :], identh[:, :]).then_inc(s["mT_ps"], 1)
                        if new:
                            project_v(t, 0)
                        if att:
                            pe.wait_ge(s["mT_ready"], b + 1)
                            scores(b, 1, q, 0, True)
                            scores(b, 1, q, 1, True)
                        if batch_in(t, bb, 1):
                            values(b - 1, 0, q, 3)
                        if new:
                            project_v(t, 1)
                        if batch_in(t, bb, 1):
                            turn_heads(b - 1)
                        if att:
                            scores(b, 1, q, 2, True)
                        if ahead:
                            pe.wait_ge(stack_ready[p], 6 * 8 * (t - p) + 6 * 16)
                            scores(b + 1, 0, p, 0, False)
                        if has(t, 0, G - 1):
                            turn_ctx(t + 1)
                        if att:
                            scores(b, 1, q, 3, True)
                            values(b, 1, q, 0)
                        if ahead:
                            scores(b + 1, 0, p, 1, False)
                        if batch_in(t, bb, 1):
                            out_product(b - 1)
                        if has(t, 0, G - 1):
                            project_k(t + 1)
                        if att:
                            values(b, 1, q, 1)
                        if att:
                            pe.wait_ge(s["exp_done"], 4 * b + 3)
                            stay_warm(psST[0], 1)
                        if ahead:
                            scores(b + 1, 0, p, 2, False)
                        if batch_in(t, bb, 2):
                            turn_xn2(b - 2, 1)
                        if att:
                            values(b, 1, q, 2)
                            stay_warm(psST[0], 2)
                        if ahead:
                            scores(b + 1, 0, p, 3, False)
                        if batch_in(t, bb, 2):
                            route(b - 2)
                        if att:
                            stay_warm(psST[0], 5)

            attention_steps(pe, step)

            pe.wait_ge(s["mask_ready"], 1)
            pe.matmul(pA[:, 0:P], trih[:, :], mask[:, :], start=True, stop=True)
            pe.matmul(pA[:, P:2 * P], onesh[:, :], mask[:, :], start=True, stop=True).then_inc(s["rank_ps"], 1)
            pe.wait_ge(s["hot_ready"], 1)
            for i in range(2 * B):
                ins = pe.matmul(pB[:, 0:3 * NS], hot_slot[:, i, :],
                                hot_val[:, i, :, :].rearrange("p v j -> p (v j)"),
                                start=(i == 0), stop=(i == 2 * B - 1))
            ins.then_inc(s["slot_ps"], 1)
            pe.wait_ge(s["w_lo"], 4 * E)
            pe.wait_ge(s["b2_moved"], 16)
            pe.wait_ge(s["routed"], 1)

            def step(t, p):
                q = 1 - p
                if has(t, 1, NT + 1):
                    e1 = pe.value_load(tile_exp[0:1, bass.ds(t - 1, 1)], min_val=0, max_val=E - 1)
                if has(t, 2, NT + 2):
                    e2 = pe.value_load(tile_exp[0:1, bass.ds(t - 2, 1)], min_val=0, max_val=E - 1)
                if has(t, 0, NT):
                    pe.wait_ge(rows_in[p], 16 * (t - p) + 32)
                    wait(pe, "gl_ready", t - 1)
                    for k in range(KT):
                        for i in range(2):
                            ins = pe.transpose((pA, pB)[p][:, (2 * k + i) * P:(2 * k + i + 1) * P],
                                               xs[p][:, i, k * P:(k + 1) * P], ident[:, :])
                    ins.then_inc(s["gT_ps"], 1)
                if has(t, 1, NT + 1):
                    j = t - 1
                    pe.wait_ge(s["gl_ready"], j + 1)
                    for u in range(4):
                        wait(pe, "gelu_done", 4 * j + u - 3)
                        for c in range(2):
                            at = (2 * u + c) * P
                            ins = split_product(banks[u][:, c * TW:(c + 1) * TW],
                                                lambda a, k: (w1h, w1l)[a][:, bass.ds(e1 * (KT * F) + k * F + at, P)],
                                                lambda a, k: xT[:, 2 * q + a, k, :])
                        ins.then_inc(s["h_ps"], 1)
                if has(t, 2, NT + 2):
                    j = t - 2
                    pe.wait_ge(s["hl_done"], 4 * j + 4)
                    wait(pe, "yy_ready", j - 1)
                    for i in range(2):
                        ps = banks[6 + p][:, i * D:(i + 1) * D]
                        pe.matmul(ps, onesh[0:2, :], b2r[:, bass.ds(e2 * D, D)], start=True, stop=False)
                        for c in range(FC):
                            for a, b_ in ((0, 0), (0, 1), (1, 0)):
                                ins = pe.matmul(ps, (hh, hl)[a][p][:, c, i * P:(i + 1) * P],
                                                (w2h, w2l)[b_][:, bass.ds(e2 * (FC * D) + c * D, D)],
                                                start=False, stop=(c == FC - 1 and a == 1))
                    ins.then_inc(s["yy_ps"], 1)

            expert_steps(pe, step)


_INS = ['x', 'ctx_1024', 'condB_tau', 'fside_BxS2_0', 'L0_xcond_Wq', 'L0_xcond_bq', 'L0_xcond_Wk', 'L0_xcond_bk',
        'L0_xcond_Wv', 'L0_xcond_bv', 'L0_xcond_Wo', 'L0_xcond_bo', 'L0_ffn_W1', 'L0_ffn_b1', 'L0_ffn_W2',
        'L0_ffn_b2', 'L0_ffn_Wr', 'L0_ffn_br']


def kernel(**inputs):
    import numpy as _np
    import concourse.bacc as _bacc
    from concourse import mybir as _mybir
    from concourse.bass_utils import run_bass_kernel_spmd as _run

    nc = _bacc.Bacc("TRN2", target_bir_lowering=False, num_devices=1)
    arrays, args = {}, []
    for name in _INS:
        a = _np.ascontiguousarray(inputs[name])
        arrays[f"in_{name}_dram"] = a
        args.append(nc.dram_tensor(f"in_{name}_dram", a.shape, _mybir.dt.from_np(a.dtype), kind="ExternalInput").ap())
    args.append(nc.dram_tensor("out_dram", (T + P, D), _mybir.dt.float32, kind="ExternalOutput").ap())
    moe_block_kernel(nc, *args)
    r = _run(nc, [arrays], core_ids=[0])
    return r.results[0]["out_dram"][0:T].reshape(B, S, D)
```
